# Optimizing a Trainium2 kernel written in Bass

```python
import numpy as np
import jax
import jax.numpy as jnp

def _softmax(x, axis=-1):
    return jax.nn.softmax(x, axis=axis)

def _gelu(x):
    return jax.nn.gelu(x, approximate=True)

def _silu(x):
    return jax.nn.silu(x)

def _sigmoid(x):
    return jax.nn.sigmoid(x)

def _layernorm(x, axis=-1, eps=1e-05):
    m = jnp.mean(x, axis=axis, keepdims=True)
    v = jnp.var(x, axis=axis, keepdims=True)
    return (x - m) / jnp.sqrt(v + eps)

def _scatter_add(tgt, idx, src, axis=0):
    return tgt.at[idx].add(src)

def _segment_sum(src, seg, n):
    return jax.ops.segment_sum(src, seg, n)
kernel_name = 'mk_adj_resnorm_d4_adj_r2_a78c4e'

def setup_inputs(seed: int=0):
    np.random.seed(seed)
    _w = jnp.asarray

    def _rec_inputs():
        import jax
        import jax.numpy as jnp
        _gk = jax.random.key(seed)
        x = -0.0002928 + 1 * jax.random.normal(jax.random.fold_in(_gk, 1), (2048, 512), jnp.float32)
        _a = jax.random.bernoulli(jax.random.fold_in(_gk, 2), 0.0078125, (2048, 2048))
        _a = jnp.logical_or(_a, jnp.swapaxes(_a, -1, -2))
        _a = jnp.logical_or(_a, jnp.eye(2048, dtype=bool))
        _af = _a.astype(jnp.float32)
        adj = _af
        return (x, adj)
    x, adj = _rec_inputs()

    def _L0_gnn_setup():
        import jax, jax.numpy as jnp
        import numpy as np
        N = 2048
        D_IN = 512
        H = 16
        DH = D_IN // H
        ALPHA = 0.2
        MASK_VAL = -65500.0
        key = jax.random.key(seed)
        ks = jax.random.split(key, 7)
        x = jax.random.normal(ks[0], (N, D_IN), dtype=jnp.float32)
        adj = jax.random.randint(ks[1], (N, N), 0, 2).astype(jnp.float32)
        s = 1.0 / np.sqrt(D_IN)
        W_seq = jax.random.normal(ks[2], (D_IN, D_IN), dtype=jnp.float32) * s
        a1 = jax.random.normal(ks[3], (DH,), dtype=jnp.float32) / np.sqrt(DH)
        a2 = jax.random.normal(ks[4], (DH,), dtype=jnp.float32) / np.sqrt(DH)
        W_out = jax.random.normal(ks[5], (D_IN, D_IN), dtype=jnp.float32) * s
        b_out = jax.random.normal(ks[6], (D_IN,), dtype=jnp.float32) * 0.01
        return {'x': x, 'adj': adj, 'W_seq': W_seq, 'a1': a1, 'a2': a2, 'W_out': W_out, 'b_out': b_out}
    _L0_gnn_all = _L0_gnn_setup()
    _L0_gnn_in = {k: v for k, v in _L0_gnn_all.items() if k in ('W_seq', 'a1', 'a2', 'W_out', 'b_out')}
    del _L0_gnn_all

    def _L1_gnn_setup():
        import jax, jax.numpy as jnp
        import numpy as np
        N = 4096
        D = 512

        def adjacent_mat(adj):
            adj = adj + jnp.eye(adj.shape[0], dtype=adj.dtype)
            deg = jnp.sum(adj, axis=1)
            dinv = jnp.where(deg > 0, deg ** (-0.5), 0.0).astype(adj.dtype)
            return dinv[:, None] * adj * dinv[None, :]
        key = jax.random.key(seed)
        k1, k2 = jax.random.split(key)
        x = jax.random.normal(k1, (N, D), dtype=jnp.float32)
        Coefficient2 = 1e-08 * jnp.ones((N, N), dtype=jnp.float32)
        A = jax.random.uniform(k2, (N, N), dtype=jnp.float32)
        return {'x': x, 'Coefficient2': Coefficient2, 'A': A}
    _L1_gnn_all = _L1_gnn_setup()
    _L1_gnn_in = {k: v for k, v in _L1_gnn_all.items() if k in ()}
    del _L1_gnn_all

    def _L2_gnn_setup():
        import jax, jax.numpy as jnp
        import numpy as np
        D_IN, D_ATTN, STEPS = (512, 64, 2)
        P_TOP, TAU, LN_EPS = (0.9, 1.0, 1e-05)
        N = 2048

        def _xavier(key, shape):
            fan_in, fan_out = (shape[0], shape[1])
            lim = jnp.sqrt(6.0 / (fan_in + fan_out))
            return jax.random.uniform(key, shape, jnp.float32, -lim, lim)

        def _adj_from_feats(Xa, W1, W2, W3):
            Q = Xa @ W1
            K = Xa @ W3
            logits = Q @ W2 @ K.T / TAU
            n = logits.shape[1]
            order = jnp.argsort(-logits, axis=1)
            vals = jnp.take_along_axis(logits, order, axis=1)
            probs = jax.nn.softmax(vals, axis=1)
            csum = jnp.cumsum(probs, axis=1)
            k_i = jnp.sum(csum < P_TOP, axis=1) + 1
            keep = jnp.arange(n)[None, :] < k_i[:, None]
            masked_sorted = jnp.where(keep, vals, -jnp.inf)
            rows = jnp.arange(n)[:, None]
            masked = jnp.full_like(logits, -jnp.inf).at[rows, order].set(masked_sorted)
            return jax.nn.softmax(masked, axis=1)
        key = jax.random.key(seed)
        ks = jax.random.split(key, 12)
        X = jax.random.normal(ks[0], (N, D_IN), jnp.float32)
        S = jax.random.uniform(ks[1], (N, N), jnp.float32)
        W1 = _xavier(ks[2], (D_IN, D_ATTN))
        W3 = _xavier(ks[3], (D_IN, D_ATTN))
        W2 = _xavier(ks[4], (D_ATTN, D_ATTN))
        U1_0 = _xavier(ks[5], (D_IN, D_IN))
        U1_1 = _xavier(ks[6], (D_IN, D_IN))
        U2_0 = _xavier(ks[7], (D_IN, D_IN))
        U2_1 = _xavier(ks[8], (D_IN, D_IN))
        gamma = jnp.ones((D_IN,), jnp.float32)
        beta = jnp.zeros((D_IN,), jnp.float32)
        return {'X': X, 'S': S, 'W1': W1, 'W2': W2, 'W3': W3, 'U1_0': U1_0, 'U1_1': U1_1, 'U2_0': U2_0, 'U2_1': U2_1, 'gamma': gamma, 'beta': beta}
    _L2_gnn_all = _L2_gnn_setup()
    _L2_gnn_in = {k: v for k, v in _L2_gnn_all.items() if k in ('W1', 'W2', 'W3', 'U1_0', 'U1_1', 'U2_0', 'U2_1', 'gamma', 'beta')}
    del _L2_gnn_all

    def _L3_gnn_setup():
        import jax, jax.numpy as jnp
        import numpy as np
        N = 4096
        IN_FEATURES = 512
        OUT_FEATURES = 512
        key = jax.random.key(seed)
        k_x, k_adj, k_w, k_b = jax.random.split(key, 4)
        x = jax.random.normal(k_x, (N, IN_FEATURES), dtype=jnp.float32)
        adj = jax.random.uniform(k_adj, (N, N), dtype=jnp.float32)
        stdv = 1.0 / np.sqrt(OUT_FEATURES)
        weight = jax.random.uniform(k_w, (IN_FEATURES, OUT_FEATURES), dtype=jnp.float32, minval=-stdv, maxval=stdv)
        bias = jax.random.uniform(k_b, (OUT_FEATURES,), dtype=jnp.float32, minval=-stdv, maxval=stdv)
        return {'x': x, 'adj': adj, 'weight': weight, 'bias': bias}
    _L3_gnn_all = _L3_gnn_setup()
    _L3_gnn_in = {k: v for k, v in _L3_gnn_all.items() if k in ('weight', 'bias')}
    del _L3_gnn_all
    return {'x': x, 'adj': adj, 'L0_gnn_W_seq': _L0_gnn_in['W_seq'], 'L0_gnn_a1': _L0_gnn_in['a1'], 'L0_gnn_a2': _L0_gnn_in['a2'], 'L0_gnn_W_out': _L0_gnn_in['W_out'], 'L0_gnn_b_out': _L0_gnn_in['b_out'], 'L2_gnn_W1': _L2_gnn_in['W1'], 'L2_gnn_W2': _L2_gnn_in['W2'], 'L2_gnn_W3': _L2_gnn_in['W3'], 'L2_gnn_U1_0': _L2_gnn_in['U1_0'], 'L2_gnn_U1_1': _L2_gnn_in['U1_1'], 'L2_gnn_U2_0': _L2_gnn_in['U2_0'], 'L2_gnn_U2_1': _L2_gnn_in['U2_1'], 'L2_gnn_gamma': _L2_gnn_in['gamma'], 'L2_gnn_beta': _L2_gnn_in['beta'], 'L3_gnn_weight': _L3_gnn_in['weight'], 'L3_gnn_bias': _L3_gnn_in['bias']}

def reference(x, adj, L0_gnn_W_seq, L0_gnn_a1, L0_gnn_a2, L0_gnn_W_out, L0_gnn_b_out, L2_gnn_W1, L2_gnn_W2, L2_gnn_W3, L2_gnn_U1_0, L2_gnn_U1_1, L2_gnn_U2_0, L2_gnn_U2_1, L2_gnn_gamma, L2_gnn_beta, L3_gnn_weight, L3_gnn_bias):
    import jax
    import jax.numpy as jnp

    def _L0_gnn_ref(x, adj, W_seq, a1, a2, W_out, b_out):
        import jax, jax.numpy as jnp
        import numpy as np
        N = 2048
        D_IN = 512
        H = 16
        DH = D_IN // H
        ALPHA = 0.2
        MASK_VAL = -65500.0
        seq = (x @ W_seq).reshape(N, H, DH)
        score1 = jnp.einsum('nhd,d->hn', seq, a1)
        score2 = jnp.einsum('nhd,d->hn', seq, a2)
        scores = score1[:, :, None] + score2[:, None, :]
        scores = jax.nn.leaky_relu(scores, negative_slope=ALPHA)
        scores = scores + (1.0 - adj)[None, :, :] * MASK_VAL
        attn = jax.nn.softmax(scores, axis=-1)
        hidden = jnp.einsum('hij,jhd->ihd', attn, seq).reshape(N, D_IN)
        hidden = hidden @ W_out + b_out
        return jax.nn.elu(hidden)

    def _L1_gnn_ref(x, Coefficient2, A):
        import jax, jax.numpy as jnp
        import numpy as np
        N = 4096
        D = 512

        def adjacent_mat(adj):
            adj = adj + jnp.eye(adj.shape[0], dtype=adj.dtype)
            deg = jnp.sum(adj, axis=1)
            dinv = jnp.where(deg > 0, deg ** (-0.5), 0.0).astype(adj.dtype)
            return dinv[:, None] * adj * dinv[None, :]
        A_c = jax.lax.stop_gradient(A)
        adj = adjacent_mat((A_c + A_c.T) * 0.5)
        y = Coefficient2 @ adj
        y = y @ x
        return y

    def _L2_gnn_ref(X, S, W1, W2, W3, U1_0, U1_1, U2_0, U2_1, gamma, beta):
        import jax, jax.numpy as jnp
        import numpy as np
        D_IN, D_ATTN, STEPS = (512, 64, 2)
        P_TOP, TAU, LN_EPS = (0.9, 1.0, 1e-05)
        N = 2048

        def _xavier(key, shape):
            fan_in, fan_out = (shape[0], shape[1])
            lim = jnp.sqrt(6.0 / (fan_in + fan_out))
            return jax.random.uniform(key, shape, jnp.float32, -lim, lim)

        def _adj_from_feats(Xa, W1, W2, W3):
            Q = Xa @ W1
            K = Xa @ W3
            logits = Q @ W2 @ K.T / TAU
            n = logits.shape[1]
            order = jnp.argsort(-logits, axis=1)
            vals = jnp.take_along_axis(logits, order, axis=1)
            probs = jax.nn.softmax(vals, axis=1)
            csum = jnp.cumsum(probs, axis=1)
            k_i = jnp.sum(csum < P_TOP, axis=1) + 1
            keep = jnp.arange(n)[None, :] < k_i[:, None]
            masked_sorted = jnp.where(keep, vals, -jnp.inf)
            rows = jnp.arange(n)[:, None]
            masked = jnp.full_like(logits, -jnp.inf).at[rows, order].set(masked_sorted)
            return jax.nn.softmax(masked, axis=1)
        n = X.shape[0]
        S = S + jnp.eye(n, dtype=X.dtype)
        R = S / jnp.clip(S.sum(axis=1, keepdims=True), 1e-12)
        Z = jnp.zeros_like(X)
        Xf, Xa = (X, X)
        U1s, U2s = ((U1_0, U1_1), (U2_0, U2_1))
        for s in range(STEPS):
            A = _adj_from_feats(Xa, W1, W2, W3)
            Xf = R @ Xf
            Xa = A @ Xa
            Z = Z + (Xf @ U1s[s] + Xa @ U2s[s])
        Y = X + Z
        mu = Y.mean(axis=-1, keepdims=True)
        var = Y.var(axis=-1, keepdims=True)
        return (Y - mu) * jax.lax.rsqrt(var + LN_EPS) * gamma + beta

    def _L3_gnn_ref(x, adj, weight, bias):
        import jax, jax.numpy as jnp
        import numpy as np
        N = 4096
        IN_FEATURES = 512
        OUT_FEATURES = 512
        support = jnp.matmul(x, weight)
        output = jnp.matmul(adj, support)
        return output + bias
    x = _layernorm(x + _L0_gnn_ref(x, adj, L0_gnn_W_seq, L0_gnn_a1, L0_gnn_a2, L0_gnn_W_out, L0_gnn_b_out), axis=-1)
    x = _layernorm(x + _L1_gnn_ref(x, adj, adj), axis=-1)
    x = _layernorm(x + _L2_gnn_ref(x, adj, L2_gnn_W1, L2_gnn_W2, L2_gnn_W3, L2_gnn_U1_0, L2_gnn_U1_1, L2_gnn_U2_0, L2_gnn_U2_1, L2_gnn_gamma, L2_gnn_beta), axis=-1)
    x = _layernorm(x + _L3_gnn_ref(x, adj, L3_gnn_weight, L3_gnn_bias), axis=-1)
    return x

_drawn_inputs = setup_inputs


def setup_inputs(seed=0):
    import zlib

    import numpy as np

    out = dict(_drawn_inputs(seed))
    spreads = {'L2_gnn_gamma': (1.0, 0.2), 'L2_gnn_beta': (0.0, 0.1)}
    factors = {'L3_gnn_bias': 36.266}
    for name, (base, spread) in spreads.items():
        noise = np.random.default_rng([zlib.crc32(name.encode()), seed]).standard_normal(out[name].shape)
        drawn = base * np.exp(spread * noise) if base else spread * noise
        out[name] = jnp.asarray(drawn.astype(out[name].dtype))
    for name, factor in factors.items():
        out[name] = (out[name] * factor).astype(out[name].dtype)
    return out
```

```python
from contextlib import ExitStack

import numpy as np

import concourse.bass as bass
from concourse import mybir

F32 = mybir.dt.float32
F16 = mybir.dt.float16
BF16 = mybir.dt.bfloat16
ALU = mybir.AluOpType
ACT = mybir.ActivationFunctionType
AX = mybir.AxisListType
RMAX = bass.bass_isa.ReduceOp.max
DS = bass.DynSlice

P = 128
N = 2048
D = 512
NT = N // P
FT = D // P
HEADS = 16
DH = D // HEADS
DC = DH + 1
QW = 512
QT = QW // P
NQ = N // QW
DA = 64
PARTS = 3
STEPS = 2
SLOPE = 0.2
EPS = 1e-5
P_TOP = 0.9
LOWEST = 2.0 ** -15
OCTAVE_STEPS = (8, 4, 2, 1)
MANTISSA_STEPS = 23
SLOTS = 2


def done(t):
    return t + 1 + SLOTS


def freed(t):
    return t + 1


def hold(eng, sem, count, held):
    eng.wait_ge(sem, count)
    eng.sem_inc(held, 1)


class Chain:

    def __init__(self, eng, sem, base=0):
        self.eng, self.sem, self.base, self.n = eng, sem, base, 0

    def link(self, ins, held=None):
        self.n += 1
        ins.then_inc(self.sem, 1)
        if held is None:
            self.eng.wait_ge(self.sem, self.base + self.n)
        else:
            hold(self.eng, self.sem, self.base + self.n, held)


def copied_by_vector(nc, out, src):
    return nc.vector.tensor_scalar(out, src, 1.0, None, ALU.mult)


class Room:

    def __init__(self, nc, offset):
        self.nc, self.at = nc, offset

    def take(self, name, shape, dtype):
        size = int(np.prod(shape[1:])) * mybir.dt.size(dtype)
        t = self.nc.alloc_sbuf_tensor_at(name, shape, dtype, offset=self.at)
        self.at += (size + 31) // 32 * 32
        assert self.at <= self.nc.sbuf_usable_end, (name, self.at)
        return t


class Kept:

    def __init__(self, nc):
        room = Room(nc, (nc.sbuf_base + 31) // 32 * 32)
        self.AT = room.take("AT", [P, NT, N], BF16)
        self.ident = room.take("ident", [P, P], F32)
        self.identb = room.take("identb", [P, P], BF16)
        self.eps = room.take("eps", [P, 1], F32)
        self.rscale = room.take("rscale", [P, NT], F32)
        self.dinv = room.take("dinv", [P, NT], F32)
        self.pool_held = nc.alloc_semaphore("pool_held")
        self.tensor_held = nc.alloc_semaphore("tensor_held")
        self.vector_held = nc.alloc_semaphore("vector_held")
        self.start = room.at
        self.X = room.take("X", [P, NT, D], F32)
        self.parts_at = room.at
        self.X3 = room.take("X3", [P, NT, PARTS, D], BF16)
        self.upper = room.at
        self.C = room.take("C", [P, NT, HEADS, DC], F32)
        self.top = room.at


def tile_rows(dram, i):
    return dram[DS(i * P, P), :]


def in_blocks(w):
    return w.rearrange("(f p) n -> p f n", p=P)


def transpose_tile(nc, out, src, ident):
    for f in range(FT):
        last = nc.tensor.transpose(out[:, f, :], src[:, f * P:(f + 1) * P], ident[:])
    return last


def project_tile(nc, out, xT, w, first=True, final=True):
    for f in range(FT):
        last = nc.tensor.matmul(out, xT[:, f, :], w[:, f, :], start=first and f == 0, stop=final and f == FT - 1)
    return last


def sum_neighbours(nc, out, AT, parts, i):
    for j in range(NT):
        for p in range(PARTS):
            last = nc.tensor.matmul(out, AT[:, j, DS(i * P, P)], parts[:, j, p, :],
                                    start=j == 0 and p == 0, stop=j == NT - 1 and p == PARTS - 1)
    return last


def split_parts(nc, ch, parts, src, rest):
    ch.link(copied_by_vector(nc, parts[:, 0, :], src))
    ch.link(nc.vector.tensor_tensor(rest, src, parts[:, 0, :], ALU.subtract))
    ch.link(copied_by_vector(nc, parts[:, 1, :], rest))
    ch.link(nc.vector.tensor_tensor(parts[:, 2, :], rest, parts[:, 1, :], ALU.subtract))


def prepare_adjacency(nc, k, adjT):
    room = Room(nc, k.start)
    raw = [room.take(f"raw{u}", [P, N], F32) for u in range(SLOTS)]
    ones = room.take("ones", [P, 1], BF16)
    colsum = room.take("colsum", [P, NT], F32)
    rowsum = room.take("rowsum", [P, NT], F32)
    deg = room.take("deg", [P, NT], F32)
    pos = room.take("pos", [P, NT], F32)
    root = room.take("root", [P, NT], F32)
    raw_in = [nc.alloc_semaphore(f"raw_in{u}") for u in range(SLOTS)]
    cast_done = nc.alloc_semaphore("cast_done")
    ones_ready = nc.alloc_semaphore("ones_ready")
    rows_summed = nc.alloc_semaphore("rows_summed")
    deg_ready = nc.alloc_semaphore("deg_ready")
    root_ready = nc.alloc_semaphore("root_ready")
    ident_made = nc.alloc_semaphore("ident_made")
    vec = nc.alloc_semaphore("prep_vec")
    with nc.psum_tensor("ps_rowsum", [P, 512], F32) as ps, nc.Block() as block:

        @block.sync
        def _(sp):
            with sp.Fori(0, NT // SLOTS) as g:
                for u in range(SLOTS):
                    sp.wait_ge(cast_done, freed(g * SLOTS + u))
                    sp.dma_start(raw[u][:], tile_rows(adjT, g * SLOTS + u)).then_inc(raw_in[u], 16)

        @block.gpsimd
        def _(pool):
            nc.gpsimd.memset(k.ident[:], 0.0).then_inc(ident_made, 1)
            pool.wait_ge(ident_made, 1)
            nc.gpsimd.affine_select(out=k.ident[:], in_=k.ident[:], compare_op=ALU.not_equal, fill=1.0, base=0,
                                    pattern=[[-1, P]], channel_multiplier=1).then_inc(ident_made, 1)
            pool.wait_ge(ident_made, 2)
            nc.gpsimd.tensor_copy(k.identb[:], k.ident[:])

        @block.scalar
        def _(act):
            act.sem_inc(cast_done, SLOTS)
            with act.Fori(0, NT // SLOTS) as g:
                for u in range(SLOTS):
                    t = g * SLOTS + u
                    act.wait_ge(raw_in[u], g * 16 + 16)
                    nc.scalar.activation(k.AT[:, t, :], raw[u][:], ACT.Copy,
                                         accum_out=colsum[:, DS(t, 1)]).then_inc(cast_done, 1)
            act.wait_ge(deg_ready, 1)
            nc.scalar.activation(root[:], deg[:], ACT.Sqrt).then_inc(root_ready, 1)

        @block.tensor
        def _(pe):
            pe.wait_ge(ones_ready, 1)
            pe.wait_ge(cast_done, done(NT - 1))
            with pe.Fori(0, NT) as i:
                for j in range(NT):
                    last = nc.tensor.matmul(ps[:, DS(i, 1)], k.AT[:, j, DS(i * P, P)], ones[:],
                                            start=j == 0, stop=j == NT - 1)
                last.then_inc(rows_summed, 1)

        @block.vector
        def _(dve):
            ch = Chain(dve, vec)
            nc.vector.memset(k.eps[:], EPS)
            nc.vector.memset(ones[:], 1.0).then_inc(ones_ready, 1)
            dve.wait_ge(rows_summed, NT)
            ch.link(nc.vector.tensor_copy(rowsum[:], ps[:, 0:NT]))
            dve.wait_ge(cast_done, done(NT - 1))
            ch.link(nc.vector.tensor_scalar(pos[:], rowsum[:], 1.0, 1e-12, ALU.add, ALU.max))
            ch.link(nc.vector.reciprocal(k.rscale[:], pos[:]))
            ch.link(nc.vector.tensor_tensor(deg[:], rowsum[:], colsum[:], ALU.add))
            ch.link(nc.vector.tensor_scalar(deg[:], deg[:], 0.5, 1.0, ALU.mult, ALU.add))
            ch.link(nc.vector.tensor_scalar(pos[:], deg[:], 0.0, None, ALU.is_gt))
            nc.vector.tensor_scalar(deg[:], deg[:], 1e-30, None, ALU.max).then_inc(deg_ready, 1)
            dve.wait_ge(root_ready, 1)
            ch.link(nc.vector.reciprocal(root[:], root[:]))
            ch.link(nc.vector.tensor_tensor(k.dinv[:], root[:], pos[:], ALU.mult))


class Gat:

    def __init__(self, nc, k):
        room = Room(nc, k.start)
        self.seq = room.take("seq", [P, NT, D], F32)
        self.u = room.take("u", [P, NT, HEADS], F32)
        self.ul = room.take("ul", [P, NT, HEADS], F32)
        self.v = room.take("v", [P, NT, HEADS], F32)
        self.vl = room.take("vl", [P, NT, HEADS], F32)
        self.minus_s2 = room.take("minus_s2", [P, NT, HEADS], F32)
        self.start = room.at


def attention_scores(nc, k, gat, x, W_seq, a1, a2, s1_rows):
    room = Room(nc, gat.start)
    w = room.take("w_seq", [P, FT, D], F32)
    a1r = room.take("a1r", [P, DH], F32)
    a2r = room.take("a2r", [P, DH], F32)
    xin = [room.take(f"sc_xin{u}", [P, D], F32) for u in range(SLOTS)]
    xT = [room.take(f"sc_xT{u}", [P, FT, P], F32) for u in range(SLOTS)]
    prod = [room.take(f"prod{u}", [P, D], F32) for u in range(2)]
    s1 = room.take("s1", [P, NT, HEADS], F32)
    s1_tile = [room.take(f"s1_tile{u}", [P, HEADS], F32) for u in range(SLOTS)]
    s2 = room.take("s2", [P, NT, HEADS], F32)
    s1T = room.take("s1T", [HEADS, N], F32)
    most = room.take("most", [P, HEADS], F32)
    most_all = room.take("most_all", [P, HEADS], F32)
    args = room.take("args", [P, 4, NT, HEADS], F32)
    w_in = nc.alloc_semaphore("sc_w_in")
    x_in = [nc.alloc_semaphore(f"sc_x_in{u}") for u in range(SLOTS)]
    x_turned = nc.alloc_semaphore("sc_x_turned")
    xT_ready = nc.alloc_semaphore("sc_xT_ready")
    seq_summed = nc.alloc_semaphore("sc_seq_summed")
    seq_kept = nc.alloc_semaphore("sc_seq_kept")
    s1_ready = nc.alloc_semaphore("sc_s1_ready")
    s1_turned = nc.alloc_semaphore("sc_s1_turned")
    s1T_ready = nc.alloc_semaphore("sc_s1T_ready")
    most_ready = nc.alloc_semaphore("sc_most_ready")
    most_all_ready = nc.alloc_semaphore("sc_most_all_ready")
    args_ready = nc.alloc_semaphore("sc_args_ready")
    s1_out = nc.alloc_semaphore("sc_s1_out")
    vec = nc.alloc_semaphore("sc_vec")
    with ExitStack() as ctx:
        psT = [ctx.enter_context(nc.psum_tensor(f"sc_psT{u}", [P, FT, P], F32)) for u in range(SLOTS)]
        psY = [ctx.enter_context(nc.psum_tensor(f"sc_psY{u}", [P, D], F32)) for u in range(SLOTS)]
        psS = [ctx.enter_context(nc.psum_tensor(f"sc_psS{u}", [P, 512], F32)) for u in range(SLOTS)]
        block = ctx.enter_context(nc.Block())

        @block.sync
        def _(sp):
            sp.dma_start(w[:], in_blocks(W_seq)).then_inc(w_in, 16)
            sp.dma_start(a1r[:], a1.partition_broadcast(P)).then_inc(w_in, 16)
            sp.dma_start(a2r[:], a2.partition_broadcast(P)).then_inc(w_in, 16)
            with sp.Fori(0, NT // SLOTS) as g:
                for u in range(SLOTS):
                    sp.wait_ge(x_turned, freed(g * SLOTS + u))
                    sp.dma_start(xin[u][:], tile_rows(x, g * SLOTS + u)).then_inc(x_in[u], 16)
            sp.wait_ge(s1T_ready, done(NT - 1))
            sp.dma_start(s1_rows, s1T[:]).then_inc(s1_out, 16)
            sp.wait_ge(s1_out, 16)

        @block.tensor
        def _(pe):
            pe.sem_inc(x_turned, SLOTS)
            pe.sem_inc(seq_summed, SLOTS)
            pe.sem_inc(s1_turned, SLOTS)
            pe.wait_ge(w_in, 48)
            with pe.Fori(0, NT // SLOTS) as g:
                for u in range(SLOTS):
                    t = g * SLOTS + u
                    pe.wait_ge(x_in[u], g * 16 + 16)
                    pe.wait_ge(xT_ready, freed(t))
                    transpose_tile(nc, psT[u], xin[u], k.ident).then_inc(x_turned, 1)
                for u in range(SLOTS):
                    t = g * SLOTS + u
                    pe.wait_ge(xT_ready, done(t))
                    pe.wait_ge(seq_kept, freed(t))
                    project_tile(nc, psY[u][:], xT[u], w).then_inc(seq_summed, 1)
                for u in range(SLOTS):
                    t = g * SLOTS + u
                    pe.wait_ge(s1_ready, t + 1)
                    pe.wait_ge(s1T_ready, freed(t))
                    nc.tensor.transpose(psS[u][0:HEADS, 0:P], s1_tile[u][:], k.ident[:]).then_inc(s1_turned, 1)

        @block.scalar
        def _(act):
            act.sem_inc(xT_ready, SLOTS)
            act.sem_inc(s1T_ready, SLOTS)
            with act.Fori(0, NT // SLOTS) as g:
                for u in range(SLOTS):
                    t = g * SLOTS + u
                    act.wait_ge(x_turned, done(t))
                    act.wait_ge(seq_summed, freed(t))
                    nc.scalar.copy(xT[u][:], psT[u][:]).then_inc(xT_ready, 1)
                for u in range(SLOTS):
                    t = g * SLOTS + u
                    act.wait_ge(s1_turned, done(t))
                    nc.scalar.copy(s1T[:, DS(t * P, P)], psS[u][0:HEADS, 0:P]).then_inc(s1T_ready, 1)
            act.wait_ge(args_ready, 1)
            for n, out in enumerate((gat.u, gat.ul, gat.v, gat.vl)):
                nc.scalar.activation(out[:], args[:, n, :, :], ACT.Exp)

        @block.gpsimd
        def _(pool):
            pool.wait_ge(most_ready, 1)
            nc.gpsimd.partition_all_reduce(most_all[:], most[:], P, RMAX).then_inc(most_all_ready, 1)

        LINKS = 4

        @block.vector
        def _(dve):
            dve.sem_inc(seq_kept, SLOTS)
            dve.wait_ge(w_in, 48)
            with dve.Fori(0, NT // SLOTS) as g:
                for u in range(SLOTS):
                    t = g * SLOTS + u
                    ch = Chain(dve, vec, t * LINKS)
                    dve.wait_ge(seq_summed, done(t))
                    copied_by_vector(nc, gat.seq[:, t, :], psY[u][:]).then_inc(seq_kept, 1)
                    dve.wait_ge(seq_kept, done(t))
                    rows = gat.seq[:, t, :].rearrange("p (h d) -> p h d", d=DH)
                    for n, a in enumerate((a1r, a2r)):
                        heads = prod[n][:].rearrange("p (h d) -> p h d", d=DH)
                        ch.link(nc.vector.tensor_tensor(heads, rows, a[:].unsqueeze(1).broadcast_to([P, HEADS, DH]),
                                                        ALU.mult))
                        if n == 0:
                            dve.wait_ge(s1_turned, freed(t))
                            nc.vector.tensor_reduce(s1_tile[u][:], heads, AX.X, ALU.add).then_inc(s1_ready, 1)
                            dve.wait_ge(s1_ready, t + 1)
                            ch.link(copied_by_vector(nc, s1[:, t, :], s1_tile[u][:]))
                        else:
                            ch.link(nc.vector.tensor_reduce(s2[:, t, :], heads, AX.X, ALU.add))
                    assert ch.n == LINKS
            dve.wait_ge(s1_ready, NT)
            ch = Chain(dve, vec, NT * LINKS)
            nc.vector.tensor_reduce(most[:], s2[:].rearrange("p t h -> p h t"), AX.X, ALU.max).then_inc(most_ready, 1)
            nc.vector.tensor_scalar(gat.minus_s2[:], s2[:], -1.0, None, ALU.mult)
            dve.wait_ge(most_all_ready, 1)
            across = most_all[:].unsqueeze(1).broadcast_to([P, NT, HEADS])
            ch.link(nc.vector.tensor_tensor(s1[:], s1[:], across, ALU.add))
            ch.link(nc.vector.tensor_tensor(s2[:], s2[:], across, ALU.subtract))
            ch.link(nc.vector.tensor_scalar(args[:, 0, :, :], s1[:], 1.0 - SLOPE, 0.0, ALU.mult, ALU.min))
            ch.link(nc.vector.tensor_scalar(args[:, 1, :, :], s1[:], SLOPE - 1.0, 0.0, ALU.mult, ALU.min))
            ch.link(copied_by_vector(nc, args[:, 2, :, :], s2[:]))
            nc.vector.tensor_scalar(args[:, 3, :, :], s2[:], SLOPE, None, ALU.mult).then_inc(args_ready, 1)


def lower_slope_sums(nc, k, gat):
    room = Room(nc, gat.start)
    V3 = [room.take(f"lo_V3_{n}", [P, NT, 2, HEADS * DC // 2], BF16) for n in range(2)]
    assert room.at <= k.upper, (room.at, k.upper)
    room = Room(nc, k.top)
    V3.append(room.take("lo_V3_2", [P, NT, 2, HEADS * DC // 2], BF16))
    whole = room.take("lo_whole", [P, HEADS, DC], F32)
    rest = room.take("lo_rest", [P, HEADS * DC], F32)
    HC = HEADS * DC // 2
    split = nc.alloc_semaphore("lo_split")
    summed = nc.alloc_semaphore("lo_summed")
    kept = nc.alloc_semaphore("lo_kept")
    with ExitStack() as ctx:
        ps = [ctx.enter_context(nc.psum_tensor(f"lo_ps{u}", [P, 2, 512], F32)) for u in range(SLOTS)]
        block = ctx.enter_context(nc.Block())
        LINKS = 6

        @block.vector
        def _(dve):
            with dve.Fori(0, NT) as t:
                ch = Chain(dve, split, t * LINKS)
                weight = gat.vl[:, t, :].unsqueeze(2)
                ch.link(nc.vector.tensor_tensor(whole[:, :, 0:DH], gat.seq[:, t, :].rearrange("p (h d) -> p h d", d=DH),
                                                weight.broadcast_to([P, HEADS, DH]), ALU.mult))
                ch.link(copied_by_vector(nc, whole[:, :, DH:DC], weight))
                parts = [v[:, t, :, :].rearrange("p c n -> p (c n)") for v in V3]
                rows = whole[:].rearrange("p h d -> p (h d)")
                ch.link(copied_by_vector(nc, parts[0], rows))
                ch.link(nc.vector.tensor_tensor(rest[:], rows, parts[0], ALU.subtract))
                ch.link(copied_by_vector(nc, parts[1], rest[:]))
                ch.link(nc.vector.tensor_tensor(parts[2], rest[:], parts[1], ALU.subtract))
                assert ch.n == LINKS

        @block.tensor
        def _(pe):
            pe.sem_inc(summed, SLOTS)
            pe.wait_ge(split, NT * LINKS)
            with pe.Fori(0, NT // SLOTS) as g:
                for u in range(SLOTS):
                    i = g * SLOTS + u
                    pe.wait_ge(kept, freed(i))
                    for j in range(NT):
                        for p in range(PARTS):
                            for c in range(2):
                                last = nc.tensor.matmul(ps[u][:, c, 0:HC], k.AT[:, j, DS(i * P, P)], V3[p][:, j, c, :],
                                                        start=j == 0 and p == 0, stop=j == NT - 1 and p == PARTS - 1)
                    last.then_inc(summed, 1)

        @block.scalar
        def _(act):
            act.sem_inc(kept, SLOTS)
            with act.Fori(0, NT // SLOTS) as g:
                for u in range(SLOTS):
                    i = g * SLOTS + u
                    act.wait_ge(summed, done(i))
                    nc.scalar.copy(k.C[:, i, :, :].rearrange("p (c h) d -> p c (h d)", c=2),
                                   ps[u][:, :, 0:HC]).then_inc(kept, 1)


def attention_heads(nc, k, gat, s1_rows):
    BOTH = 2 * DC
    room = Room(nc, gat.start)
    B = [room.take(f"B{u}", [P, NT, QW], BF16) for u in range(SLOTS)]
    V3 = [room.take("hd_V3_0", [P, NT, PARTS * BOTH], BF16)]
    assert room.at <= k.upper, (room.at, k.upper)
    room = Room(nc, k.top)
    V3.append(room.take("hd_V3_1", [P, NT, PARTS * BOTH], BF16))
    s1b = [room.take(f"s1b{q}", [P, QW], F32) for q in range(2)]
    whole = room.take("hd_whole", [P, NT, BOTH], F32)
    raw = [room.take(f"hd_raw{u}", [P, QT, PARTS, BOTH], F32) for u in range(SLOTS)]
    sums = room.take("hd_sums", [P, QT, BOTH], F32)
    s1_in = [nc.alloc_semaphore(f"hd_s1_in{u}") for u in range(SLOTS)]
    masked = nc.alloc_semaphore("hd_masked")
    summed = nc.alloc_semaphore("hd_summed")
    copied = nc.alloc_semaphore("hd_copied")
    added = nc.alloc_semaphore("hd_added")
    v_split = nc.alloc_semaphore("hd_v_split")
    pool_steps = nc.alloc_semaphore("hd_pool_steps")
    with ExitStack() as ctx:
        ps = [ctx.enter_context(nc.psum_tensor(f"hd_ps{u}", [P, 2, 512], F32)) for u in range(SLOTS)]
        block = ctx.enter_context(nc.Block())

        @block.sync
        def _(sp):
            with sp.Fori(0, HEADS) as h:
                for q in range(NQ):
                    sp.wait_ge(masked, freed(h * NQ + q))
                    sp.dma_start(s1b[q % 2][:], s1_rows[h, q * QW:(q + 1) * QW].partition_broadcast(P)
                                 ).then_inc(s1_in[q % 2], 16)

        @block.vector
        def _(dve):
            dve.sem_inc(masked, SLOTS)
            with dve.Fori(0, HEADS) as h:
                for q in range(NQ):
                    dve.wait_ge(s1_in[q % 2], h * (16 * NQ // 2) + 16 * (q // 2 + 1))
                    dve.wait_ge(summed, freed(h * NQ + q))
                    for j in range(NT):
                        last = nc.vector.scalar_tensor_tensor(
                            B[q % 2][:, j, :], s1b[q % 2][:], gat.minus_s2[:, j, DS(h, 1)],
                            k.AT[:, j, q * QW:(q + 1) * QW], ALU.is_ge, ALU.mult)
                    last.then_inc(masked, 1)

        @block.tensor
        def _(pe):
            pe.sem_inc(summed, SLOTS)
            with pe.Fori(0, HEADS // 2) as g:
                for v in range(2):
                    h = g * 2 + v
                    pe.wait_ge(v_split, h + 1)
                    for q in range(NQ):
                        pe.wait_ge(masked, done(h * NQ + q))
                        pe.wait_ge(copied, freed(h * NQ + q))
                        for i in range(QT):
                            for j in range(NT):
                                last = nc.tensor.matmul(
                                    ps[q % 2][:, i // 2, (i % 2) * PARTS * BOTH:(i % 2 + 1) * PARTS * BOTH],
                                    B[q % 2][:, j, i * P:(i + 1) * P], V3[v][:, j, :], start=j == 0, stop=j == NT - 1)
                        last.then_inc(summed, 1)

        @block.scalar
        def _(act):
            act.sem_inc(copied, SLOTS)
            with act.Fori(0, HEADS) as h:
                for q in range(NQ):
                    Q = h * NQ + q
                    act.wait_ge(summed, done(Q))
                    act.wait_ge(added, freed(Q))
                    nc.scalar.copy(raw[q % 2][:].rearrange("p (b i) a c -> p b (i a c)", b=2),
                                   ps[q % 2][:, :, 0:2 * PARTS * BOTH]).then_inc(copied, 1)

        V_LINKS = 7
        Q_LINKS = 5
        H_LINKS = V_LINKS + NQ * Q_LINKS

        @block.gpsimd
        def _(pool):
            def split_v(h, v, base):
                ch = Chain(pool, pool_steps, base)
                rows = gat.seq[:, :, DS(h * DH, DH)]
                for n, weights in enumerate((gat.v, gat.vl)):
                    weight = weights[:, :, DS(h, 1)]
                    ch.link(nc.gpsimd.tensor_tensor(whole[:, :, n * DC:n * DC + DH], rows,
                                                    weight.broadcast_to([P, NT, DH]), ALU.mult), k.pool_held)
                    ch.link(nc.gpsimd.tensor_copy(whole[:, :, n * DC + DH:(n + 1) * DC], weight), k.pool_held)
                parts = [V3[v][:, :, a * BOTH:(a + 1) * BOTH] for a in range(PARTS)]
                ch.link(nc.gpsimd.tensor_copy(parts[0], whole[:]), k.pool_held)
                ch.link(nc.gpsimd.tensor_tensor(whole[:], whole[:], parts[0], ALU.subtract), k.pool_held)
                ch.link(nc.gpsimd.tensor_copy(parts[1], whole[:]), k.pool_held)
                assert ch.n == V_LINKS
                nc.gpsimd.tensor_tensor(parts[2], whole[:], parts[1], ALU.subtract).then_inc(v_split, 1)
                hold(pool, v_split, h + 1, k.pool_held)

            def combine(h, base):
                ch = Chain(pool, pool_steps, base)
                for q in range(NQ):
                    Q = h * NQ + q
                    hold(pool, copied, done(Q), k.pool_held)
                    ch.link(nc.gpsimd.tensor_tensor(sums[:], raw[q % 2][:, :, 0, :], raw[q % 2][:, :, 1, :], ALU.add), k.pool_held)
                    nc.gpsimd.tensor_tensor(sums[:], sums[:], raw[q % 2][:, :, 2, :], ALU.add).then_inc(added, 1)
                    hold(pool, added, done(Q), k.pool_held)
                    tiles = slice(q * QT, (q + 1) * QT)
                    C = k.C[:, tiles, h, :]
                    up, low = sums[:, :, 0:DC], sums[:, :, DC:BOTH]
                    u = gat.u[:, tiles, DS(h, 1)].broadcast_to([P, QT, DC])
                    ul = gat.ul[:, tiles, DS(h, 1)].broadcast_to([P, QT, DC])
                    ch.link(nc.gpsimd.tensor_tensor(low, C, low, ALU.subtract), k.pool_held)
                    ch.link(nc.gpsimd.tensor_tensor(low, low, ul, ALU.mult), k.pool_held)
                    ch.link(nc.gpsimd.tensor_tensor(up, up, u, ALU.mult), k.pool_held)
                    ch.link(nc.gpsimd.tensor_tensor(C, up, low, ALU.add), k.pool_held)
                assert ch.n == NQ * Q_LINKS

            pool.sem_inc(added, SLOTS)
            split_v(0, 0, 0)
            split_v(1, 1, V_LINKS)
            with pool.Fori(0, HEADS // 2 - 1) as g:
                for v in range(2):
                    h = g * 2 + v
                    base = h * H_LINKS + 2 * V_LINKS
                    combine(h, base)
                    split_v(h + 2, v, base + NQ * Q_LINKS)
            for h in (HEADS - 2, HEADS - 1):
                combine(h, (HEADS - 2) * H_LINKS + 2 * V_LINKS + (h - HEADS + 2) * NQ * Q_LINKS)


def attention_output(nc, k, x, W_out, b_out, x1):
    room = Room(nc, k.top)
    w = room.take("w_out", [P, FT, D], F32)
    bias = room.take("ao_bias", [P, D], F32)
    xin = [room.take(f"ao_x{u}", [P, D], F32) for u in range(SLOTS)]
    hid = room.take("ao_hid", [P, D], F32)
    hT = room.take("ao_hT", [P, FT, P], F32)
    rden = room.take("ao_rden", [P, HEADS], F32)
    low = room.take("ao_low", [P, D], F32)
    stats = room.take("ao_stats", [P, 6], F32)
    mv = room.take("ao_mv", [P, 2], F32)
    sd = room.take("ao_sd", [P, 1], F32)
    rstd = room.take("ao_rstd", [P, 1], F32)
    w_in = nc.alloc_semaphore("ao_w_in")
    x_in = [nc.alloc_semaphore(f"ao_x_in{u}") for u in range(SLOTS)]
    hid_ready = nc.alloc_semaphore("ao_hid_ready")
    turned = nc.alloc_semaphore("ao_turned")
    hT_ready = nc.alloc_semaphore("ao_hT_ready")
    summed = nc.alloc_semaphore("ao_summed")
    low_ready = nc.alloc_semaphore("ao_low_ready")
    exp_done = nc.alloc_semaphore("ao_exp_done")
    var_ready = nc.alloc_semaphore("ao_var_ready")
    root_ready = nc.alloc_semaphore("ao_root_ready")
    x1_ready = nc.alloc_semaphore("ao_x1_ready")
    x1_out = [nc.alloc_semaphore(f"ao_x1_out{u}") for u in range(SLOTS)]
    vec = nc.alloc_semaphore("ao_vec")
    with ExitStack() as ctx:
        psT = ctx.enter_context(nc.psum_tensor("ao_psT", [P, FT, P], F32))
        psY = ctx.enter_context(nc.psum_tensor("ao_psY", [P, D], F32))
        block = ctx.enter_context(nc.Block())

        @block.sync
        def _(sp):
            sp.dma_start(w[:], in_blocks(W_out)).then_inc(w_in, 16)
            sp.dma_start(bias[:], b_out.partition_broadcast(P)).then_inc(w_in, 16)
            for u in range(SLOTS):
                sp.dma_start(xin[u][:], tile_rows(x, u)).then_inc(x_in[u], 16)
            with sp.Fori(0, NT // SLOTS - 1) as g:
                for u in range(SLOTS):
                    t = g * SLOTS + u
                    sp.wait_ge(x1_ready, t + 1)
                    sp.dma_start(tile_rows(x1, t), xin[u][:]).then_inc(x1_out[u], 16)
                    sp.wait_ge(x1_out[u], g * 16 + 16)
                    sp.dma_start(xin[u][:], tile_rows(x, t + SLOTS)).then_inc(x_in[u], 16)
            for u in range(SLOTS):
                t = NT - SLOTS + u
                sp.wait_ge(x1_ready, t + 1)
                sp.dma_start(tile_rows(x1, t), xin[u][:]).then_inc(x1_out[u], 16)
            for u in range(SLOTS):
                sp.wait_ge(x1_out[u], 16 * NT // SLOTS)

        @block.tensor
        def _(pe):
            pe.wait_ge(w_in, 32)
            with pe.Fori(0, NT) as t:
                pe.wait_ge(hid_ready, t + 1)
                transpose_tile(nc, psT, hid, k.ident).then_inc(turned, 1)
                pe.wait_ge(hT_ready, t + 1)
                project_tile(nc, psY[:], hT, w).then_inc(summed, 1)

        @block.scalar
        def _(act):
            with act.Fori(0, NT) as t:
                act.wait_ge(turned, t + 1)
                nc.scalar.copy(hT[:], psT[:]).then_inc(hT_ready, 1)
                act.wait_ge(low_ready, t + 1)
                nc.scalar.activation(low[:], low[:], ACT.Exp).then_inc(exp_done, 1)
                act.wait_ge(var_ready, t + 1)
                nc.scalar.activation(sd[:], mv[:, 1:2], ACT.Sqrt, bias=k.eps[:]).then_inc(root_ready, 1)

        LINKS = 11

        @block.vector
        def _(dve):
            dve.wait_ge(w_in, 32)
            with dve.Fori(0, NT // SLOTS) as g:
                for u in range(SLOTS):
                    t = g * SLOTS + u
                    ch = Chain(dve, vec, t * LINKS)
                    ch.link(nc.vector.reciprocal(rden[:].unsqueeze(2), k.C[:, t, :, DH:DC]))
                    nc.vector.tensor_tensor(hid[:].rearrange("p (h d) -> p h d", d=DH), k.C[:, t, :, 0:DH],
                                            rden[:].unsqueeze(2).broadcast_to([P, HEADS, DH]),
                                            ALU.mult).then_inc(hid_ready, 1)
                    dve.wait_ge(summed, t + 1)
                    ch.link(nc.vector.tensor_tensor(hid[:], psY[:], bias[:], ALU.add))
                    nc.vector.tensor_scalar(low[:], hid[:], 0.0, None, ALU.min).then_inc(low_ready, 1)
                    dve.wait_ge(x_in[u], g * 16 + 16)
                    ch.link(nc.vector.scalar_tensor_tensor(hid[:], hid[:], 0.0, xin[u][:], ALU.max, ALU.add))
                    dve.wait_ge(exp_done, t + 1)
                    ch.link(nc.vector.scalar_tensor_tensor(hid[:], low[:], -1.0, hid[:], ALU.add, ALU.add))
                    ch.link(nc.vector.bn_stats(stats[:], hid[:]), k.vector_held)
                    nc.vector.bn_aggr(mv[:], stats[:]).then_inc(var_ready, 1)
                    dve.wait_ge(root_ready, t + 1)
                    ch.link(nc.vector.reciprocal(rstd[:], sd[:]))
                    ch.link(nc.vector.tensor_scalar(xin[u][:], hid[:], mv[:, 0:1], rstd[:], ALU.subtract, ALU.mult))
                    nc.vector.tensor_scalar(k.X[:, t, :], xin[u][:], k.dinv[:, DS(t, 1)], None,
                                            ALU.mult).then_inc(x1_ready, 1)
                    dve.wait_ge(x1_ready, t + 1)
                    split_parts(nc, ch, k.X3[:, t, :, :], k.X[:, t, :], low[:])
                    assert ch.n == LINKS


def normalised_sum(nc, k, adj):
    HN = N // 2
    room = Room(nc, k.upper)
    S = room.take("S", [P, NT, HN], BF16)
    raw = [room.take(f"ns_raw{u}", [P, HN], F32) for u in range(SLOTS)]
    tmp = room.take("ns_tmp", [P, D], F32)
    raw_in = [nc.alloc_semaphore(f"ns_raw_in{u}") for u in range(SLOTS)]
    made = nc.alloc_semaphore("ns_made")
    summed = nc.alloc_semaphore("ns_summed")
    kept = nc.alloc_semaphore("ns_kept")
    vec = nc.alloc_semaphore("ns_vec")
    with ExitStack() as ctx:
        ps = [ctx.enter_context(nc.psum_tensor(f"ns_ps{u}", [P, D], F32)) for u in range(SLOTS)]
        block = ctx.enter_context(nc.Block())

        @block.sync
        def _(sp):
            for half in range(2):
                with sp.Fori(0, NT // SLOTS) as g:
                    for u in range(SLOTS):
                        t = g * SLOTS + u
                        sp.wait_ge(made, freed(t + half * NT))
                        sp.dma_start(raw[u][:], adj[DS(t * P, P), half * HN:(half + 1) * HN]).then_inc(raw_in[u], 16)

        @block.gpsimd
        def _(pool):
            pool.sem_inc(made, SLOTS)
            for half in range(2):
                if half:
                    pool.wait_ge(summed, done(NT // 2 - 1))
                with pool.Fori(0, NT // SLOTS) as g:
                    for u in range(SLOTS):
                        t = g * SLOTS + u
                        hold(pool, raw_in[u], g * 16 + 16 + half * 8 * NT, k.pool_held)
                        nc.gpsimd.tensor_tensor(S[:, t, :], raw[u][:], k.AT[:, t, half * HN:(half + 1) * HN],
                                                ALU.add).then_inc(made, 1)

        @block.tensor
        def _(pe):
            pe.sem_inc(summed, SLOTS)
            for half in range(2):
                pe.wait_ge(made, done((half + 1) * NT - 1))
                with pe.Fori(0, NT // 2 // SLOTS) as g:
                    for u in range(SLOTS):
                        t = g * SLOTS + u
                        pe.wait_ge(kept, freed(t + half * (NT // 2)))
                        sum_neighbours(nc, ps[u][:], S, k.X3, t).then_inc(summed, 1)

        @block.vector
        def _(dve):
            dve.sem_inc(kept, SLOTS)
            for half in range(2):
                with dve.Fori(0, NT // 2 // SLOTS) as g:
                    for u in range(SLOTS):
                        t = g * SLOTS + u + half * (NT // 2)
                        ch = Chain(dve, vec, t)
                        dve.wait_ge(summed, done(t))
                        ch.link(nc.vector.scalar_tensor_tensor(tmp[:], ps[u][:], 0.5, k.X[:, t, :], ALU.mult, ALU.add))
                        nc.vector.tensor_scalar(k.X[:, t, :], tmp[:], k.dinv[:, DS(t, 1)], None,
                                                ALU.mult).then_inc(kept, 1)
                        dve.wait_ge(kept, done(t))


def split_rows(nc, k, name):
    room = Room(nc, k.upper)
    rest = room.take(f"{name}_rest", [P, D], F32)
    vec = nc.alloc_semaphore(f"{name}_vec")
    LINKS = 4
    with nc.Block() as block:

        @block.vector
        def _(dve):
            with dve.Fori(0, NT) as t:
                split_parts(nc, Chain(dve, vec, t * LINKS), k.X3[:, t, :, :], k.X[:, t, :], rest[:])


def sum_and_normalise(nc, k, name, base, bias_row, out, keep):
    room = Room(nc, k.upper)
    rows = [room.take(f"{name}_rows{u}", [P, D], F32) for u in range(SLOTS)]
    bias = room.take(f"{name}_bias", [P, D], F32)
    stats = room.take(f"{name}_stats", [P, 6], F32)
    mv = room.take(f"{name}_mv", [P, 2], F32)
    sd = room.take(f"{name}_sd", [P, 1], F32)
    rstd = room.take(f"{name}_rstd", [P, 1], F32)
    bias_in = nc.alloc_semaphore(f"{name}_bias_in")
    rows_in = [nc.alloc_semaphore(f"{name}_rows_in{u}") for u in range(SLOTS)]
    rows_out = [nc.alloc_semaphore(f"{name}_rows_out{u}") for u in range(SLOTS)]
    summed = nc.alloc_semaphore(f"{name}_summed")
    added = nc.alloc_semaphore(f"{name}_added")
    var_ready = nc.alloc_semaphore(f"{name}_var_ready")
    root_ready = nc.alloc_semaphore(f"{name}_root_ready")
    out_ready = nc.alloc_semaphore(f"{name}_out_ready")
    vec = nc.alloc_semaphore(f"{name}_vec")
    with ExitStack() as ctx:
        ps = [ctx.enter_context(nc.psum_tensor(f"{name}_ps{u}", [P, D], F32)) for u in range(SLOTS)]
        block = ctx.enter_context(nc.Block())

        @block.sync
        def _(sp):
            if bias_row is not None:
                sp.dma_start(bias[:], bias_row.partition_broadcast(P)).then_inc(bias_in, 16)
            for u in range(SLOTS):
                sp.dma_start(rows[u][:], tile_rows(base, u)).then_inc(rows_in[u], 16)
            with sp.Fori(0, NT // SLOTS - 1) as g:
                for u in range(SLOTS):
                    t = g * SLOTS + u
                    sp.wait_ge(out_ready, t + 1)
                    sp.dma_start(tile_rows(out, t), rows[u][:]).then_inc(rows_out[u], 16)
                    sp.wait_ge(rows_out[u], g * 16 + 16)
                    sp.dma_start(rows[u][:], tile_rows(base, t + SLOTS)).then_inc(rows_in[u], 16)
            for u in range(SLOTS):
                t = NT - SLOTS + u
                sp.wait_ge(out_ready, t + 1)
                sp.dma_start(tile_rows(out, t), rows[u][:]).then_inc(rows_out[u], 16)
            for u in range(SLOTS):
                sp.wait_ge(rows_out[u], 16 * NT // SLOTS)

        @block.tensor
        def _(pe):
            with pe.Fori(0, NT // SLOTS) as g:
                for u in range(SLOTS):
                    t = g * SLOTS + u
                    pe.wait_ge(added, freed(t))
                    sum_neighbours(nc, ps[u][:], k.AT, k.X3, t).then_inc(summed, 1)

        @block.scalar
        def _(act):
            with act.Fori(0, NT) as t:
                act.wait_ge(var_ready, t + 1)
                nc.scalar.activation(sd[:], mv[:, 1:2], ACT.Sqrt, bias=k.eps[:]).then_inc(root_ready, 1)

        LINKS = 2 + (bias_row is not None) + keep

        @block.vector
        def _(dve):
            dve.sem_inc(added, SLOTS)
            if bias_row is not None:
                dve.wait_ge(bias_in, 16)
            with dve.Fori(0, NT // SLOTS) as g:
                for u in range(SLOTS):
                    t = g * SLOTS + u
                    ch = Chain(dve, vec, t * LINKS)
                    dve.wait_ge(rows_in[u], g * 16 + 16)
                    if bias_row is not None:
                        ch.link(nc.vector.tensor_tensor(rows[u][:], rows[u][:], bias[:], ALU.add))
                    dve.wait_ge(summed, t + 1)
                    nc.vector.tensor_tensor(rows[u][:], rows[u][:], ps[u][:], ALU.add).then_inc(added, 1)
                    dve.wait_ge(added, done(t))
                    ch.link(nc.vector.bn_stats(stats[:], rows[u][:]), k.vector_held)
                    nc.vector.bn_aggr(mv[:], stats[:]).then_inc(var_ready, 1)
                    dve.wait_ge(root_ready, t + 1)
                    ch.link(nc.vector.reciprocal(rstd[:], sd[:]))
                    normal = nc.vector.tensor_scalar(rows[u][:], rows[u][:], mv[:, 0:1], rstd[:], ALU.subtract, ALU.mult)
                    if keep:
                        ch.link(normal)
                        normal = copied_by_vector(nc, k.X[:, t, :], rows[u][:])
                    normal.then_inc(out_ready, 1)
                    assert ch.n == LINKS


def logit_factors(nc, k, s, kT, Xf, Xa, W1, W2, W3, q_rows):
    room = Room(nc, k.after_kT)
    w1 = room.take(f"lf{s}_w1", [P, FT, DA], F32)
    w2 = room.take(f"lf{s}_w2", [DA, DA], F32)
    w3 = room.take(f"lf{s}_w3", [P, FT, DA], F32)
    xf = [room.take(f"lf{s}_xf{u}", [P, D], F32) for u in range(SLOTS)]
    xa = [room.take(f"lf{s}_xa{u}", [P, D], F32) for u in range(SLOTS)]
    xT = [room.take(f"lf{s}_xT{u}", [P, FT, P], F32) for u in range(SLOTS)]
    q0 = [room.take(f"lf{s}_q0{u}", [DA, P], F32) for u in range(SLOTS)]
    q2 = room.take(f"lf{s}_q2", [DA, N], F32)
    rest = room.take(f"lf{s}_rest", [P, D], F32)
    w_in = nc.alloc_semaphore(f"lf{s}_w_in")
    X_in = nc.alloc_semaphore(f"lf{s}_X_in")
    xf_in = [nc.alloc_semaphore(f"lf{s}_xf_in{u}") for u in range(SLOTS)]
    xa_in = [nc.alloc_semaphore(f"lf{s}_xa_in{u}") for u in range(SLOTS)]
    split = nc.alloc_semaphore(f"lf{s}_split")
    turned = nc.alloc_semaphore(f"lf{s}_turned")
    xT_ready = nc.alloc_semaphore(f"lf{s}_xT_ready")
    kq_summed = nc.alloc_semaphore(f"lf{s}_kq_summed")
    q0_ready = nc.alloc_semaphore(f"lf{s}_q0_ready")
    q2_summed = nc.alloc_semaphore(f"lf{s}_q2_summed")
    q2_ready = nc.alloc_semaphore(f"lf{s}_q2_ready")
    q2_out = nc.alloc_semaphore(f"lf{s}_q2_out")
    vec = nc.alloc_semaphore(f"lf{s}_vec")
    with ExitStack() as ctx:
        psT = [ctx.enter_context(nc.psum_tensor(f"lf{s}_psT{u}", [P, FT, P], F32)) for u in range(SLOTS)]
        psK = [ctx.enter_context(nc.psum_tensor(f"lf{s}_psK{u}", [P, 512], F32)) for u in range(SLOTS)]
        psQ = [ctx.enter_context(nc.psum_tensor(f"lf{s}_psQ{u}", [P, 512], F32)) for u in range(SLOTS)]
        psR = [ctx.enter_context(nc.psum_tensor(f"lf{s}_psR{u}", [P, 512], F32)) for u in range(SLOTS)]
        block = ctx.enter_context(nc.Block())

        @block.sync
        def _(sp):
            sp.dma_start(w1[:], in_blocks(W1)).then_inc(w_in, 16)
            sp.dma_start(w3[:], in_blocks(W3)).then_inc(w_in, 16)
            sp.dma_start(w2[:], W2).then_inc(w_in, 16)
            with sp.Fori(0, NT // SLOTS) as g:
                for u in range(SLOTS):
                    t = g * SLOTS + u
                    sp.wait_ge(turned, freed(t))
                    sp.dma_start(xa[u][:], tile_rows(Xa, t)).then_inc(xa_in[u], 16)
                    sp.wait_ge(split, freed(t))
                    sp.dma_start(xf[u][:], tile_rows(Xf, t)).then_inc(xf_in[u], 16)
            sp.dma_start(k.X[:], Xa.rearrange("(t p) d -> p t d", p=P)).then_inc(X_in, 16)
            sp.wait_ge(q2_ready, done(NT - 1))
            sp.dma_start(q_rows, q2[:]).then_inc(q2_out, 16)
            sp.wait_ge(q2_out, 16)
            sp.wait_ge(X_in, 16)

        @block.tensor
        def _(pe):
            pe.sem_inc(turned, SLOTS)
            pe.sem_inc(kq_summed, SLOTS)
            pe.sem_inc(q2_summed, SLOTS)
            pe.wait_ge(w_in, 48)
            with pe.Fori(0, NT // SLOTS) as g:
                for u in range(SLOTS):
                    t = g * SLOTS + u
                    pe.wait_ge(xa_in[u], g * 16 + 16)
                    pe.wait_ge(xT_ready, freed(t))
                    transpose_tile(nc, psT[u], xa[u], k.ident).then_inc(turned, 1)
                for u in range(SLOTS):
                    t = g * SLOTS + u
                    pe.wait_ge(xT_ready, done(t))
                    pe.wait_ge(q0_ready, freed(t))
                    for w, ps in ((w3, psK[u]), (w1, psQ[u])):
                        for f in range(FT):
                            last = nc.tensor.matmul(ps[0:DA, 0:P], w[:, f, :], xT[u][:, f, :],
                                                    start=f == 0, stop=f == FT - 1)
                    last.then_inc(kq_summed, 1)
                for u in range(SLOTS):
                    t = g * SLOTS + u
                    pe.wait_ge(q0_ready, done(t))
                    hold(pe, q2_ready, freed(t), k.tensor_held)
                    nc.tensor.matmul(psR[u][0:DA, 0:P], w2[:], q0[u][:], start=True, stop=True).then_inc(q2_summed, 1)

        @block.scalar
        def _(act):
            act.sem_inc(xT_ready, SLOTS)
            act.sem_inc(q0_ready, SLOTS)
            act.sem_inc(q2_ready, SLOTS)
            with act.Fori(0, NT // SLOTS) as g:
                for u in range(SLOTS):
                    t = g * SLOTS + u
                    act.wait_ge(turned, done(t))
                    act.wait_ge(kq_summed, freed(t))
                    nc.scalar.copy(xT[u][:], psT[u][:]).then_inc(xT_ready, 1)
                for u in range(SLOTS):
                    t = g * SLOTS + u
                    act.wait_ge(kq_summed, done(t))
                    nc.scalar.copy(kT[:, DS(t * P, P)], psK[u][0:DA, 0:P])
                    act.wait_ge(q2_summed, freed(t))
                    nc.scalar.copy(q0[u][:], psQ[u][0:DA, 0:P]).then_inc(q0_ready, 1)
                for u in range(SLOTS):
                    t = g * SLOTS + u
                    act.wait_ge(q2_summed, done(t))
                    nc.scalar.copy(q2[:, DS(t * P, P)], psR[u][0:DA, 0:P]).then_inc(q2_ready, 1)

        LINKS = 3

        @block.vector
        def _(dve):
            dve.sem_inc(split, SLOTS)
            with dve.Fori(0, NT // SLOTS) as g:
                for u in range(SLOTS):
                    t = g * SLOTS + u
                    dve.wait_ge(xf_in[u], g * 16 + 16)
                    ch = Chain(dve, vec, t * LINKS)
                    parts = k.X3[:, t, :, :]
                    ch.link(copied_by_vector(nc, parts[:, 0, :], xf[u][:]))
                    ch.link(nc.vector.tensor_tensor(rest[:], xf[u][:], parts[:, 0, :], ALU.subtract))
                    ch.link(copied_by_vector(nc, parts[:, 1, :], rest[:]))
                    nc.vector.tensor_tensor(parts[:, 2, :], rest[:], parts[:, 1, :], ALU.subtract).then_inc(split, 1)
                    dve.wait_ge(split, done(t))


def nucleus_step(nc, k, s, kT, q_rows, Xf_next, Xa_next):
    room = Room(nc, k.after_kT)
    PAIR = 2
    E = [[room.take(f"nu{s}_E{v}{a}", [P, N], F32) for a in range(PAIR)] for v in range(SLOTS)]
    WT = room.take(f"nu{s}_WT", [P, NT, P], F32)
    tie = room.take(f"nu{s}_tie", [P, N], BF16)
    rank = room.take(f"nu{s}_rank", [P, N], F16)
    qT = [room.take(f"nu{s}_qT{u}", [DA, P], F32) for u in range(SLOTS)]
    xf_out = room.take(f"nu{s}_xf_out", [P, D], F32)
    xa_out = room.take(f"nu{s}_xa_out", [P, D], F32)
    top = room.take(f"nu{s}_top", [P, NT], F32)
    minus_top = room.take(f"nu{s}_minus_top", [P, NT], F32)
    mass = room.take(f"nu{s}_mass", [P, NT], F32)
    rnorm = room.take(f"nu{s}_rnorm", [P, NT], F32)
    small = room.take(f"nu{s}_small", [P, 10, PAIR], F32)
    goal, low, mid, step, above, over, tmp, count, most, one = [small[:, n, :] for n in range(10)]
    qT_in = [nc.alloc_semaphore(f"nu{s}_qT_in{u}") for u in range(SLOTS)]
    logits_summed = nc.alloc_semaphore(f"nu{s}_logits_summed")
    top_ready = nc.alloc_semaphore(f"nu{s}_top_ready")
    exp_done = nc.alloc_semaphore(f"nu{s}_exp_done")
    xf_summed = nc.alloc_semaphore(f"nu{s}_xf_summed")
    xf_copied = nc.alloc_semaphore(f"nu{s}_xf_copied")
    xf_stored = nc.alloc_semaphore(f"nu{s}_xf_stored")
    weights_ready = nc.alloc_semaphore(f"nu{s}_weights_ready")
    turned = nc.alloc_semaphore(f"nu{s}_turned")
    WT_ready = nc.alloc_semaphore(f"nu{s}_WT_ready")
    xa_summed = nc.alloc_semaphore(f"nu{s}_xa_summed")
    xa_copied = nc.alloc_semaphore(f"nu{s}_xa_copied")
    xa_stored = nc.alloc_semaphore(f"nu{s}_xa_stored")
    vec = nc.alloc_semaphore(f"nu{s}_vec")
    probed = nc.alloc_semaphore(f"nu{s}_probed")
    NP = NT // PAIR
    GROUPS = NT // 4
    with ExitStack() as ctx:
        psL = ctx.enter_context(nc.psum_tensor(f"nu{s}_psL", [P, N], F32))
        psF = ctx.enter_context(nc.psum_tensor(f"nu{s}_psF", [P, D], F32))
        psA = ctx.enter_context(nc.psum_tensor(f"nu{s}_psA", [P, D], F32))
        psT = [ctx.enter_context(nc.psum_tensor(f"nu{s}_psT{u}", [P, 4, P], F32)) for u in range(SLOTS)]
        block = ctx.enter_context(nc.Block())

        @block.sync
        def _(sp):
            def load_q(p):
                for a in range(PAIR):
                    t = p * PAIR + a
                    sp.wait_ge(logits_summed, freed(t))
                    sp.dma_start(qT[a][:], q_rows[:, DS(t * P, P)]).then_inc(qT_in[a], 16)

            def store(p):
                for a in range(PAIR):
                    t = p * PAIR + a
                    sp.wait_ge(xf_copied, t + 2)
                    sp.dma_start(tile_rows(Xf_next, t), xf_out[:]).then_inc(xf_stored, 16)
                for a in range(PAIR):
                    t = p * PAIR + a
                    sp.wait_ge(xa_copied, t + 2)
                    sp.dma_start(tile_rows(Xa_next, t), xa_out[:]).then_inc(xa_stored, 16)

            sp.sem_inc(xf_stored, 16)
            sp.sem_inc(xa_stored, 16)
            load_q(0)
            with sp.Fori(0, NP - 1) as p:
                load_q(p + 1)
                store(p)
            store(NP - 1)
            sp.wait_ge(xf_stored, 16 * (NT + 1))
            sp.wait_ge(xa_stored, 16 * (NT + 1))

        @block.tensor
        def _(pe):
            def logits(p):
                for a in range(PAIR):
                    t = p * PAIR + a
                    pe.wait_ge(qT_in[a], p * 16 + 16)
                    pe.wait_ge(exp_done, t + 1)
                    for c in range(NQ):
                        last = nc.tensor.matmul(psL[:, c * 512:(c + 1) * 512], qT[a][:], kT[:, c * 512:(c + 1) * 512],
                                                start=True, stop=True)
                    last.then_inc(logits_summed, 1)

            def neighbours(p):
                for a in range(PAIR):
                    t = p * PAIR + a
                    pe.wait_ge(xf_copied, t + 1)
                    for n in range(PARTS):
                        nc.tensor.matmul(psF[:], k.identb[:], k.X3[:, t, n, :], start=n == 0, stop=False)
                    for j in range(NT):
                        for n in range(PARTS):
                            last = nc.tensor.matmul(psF[:], k.AT[:, j, DS(t * P, P)], k.X3[:, j, n, :],
                                                    start=False, stop=j == NT - 1 and n == PARTS - 1)
                    last.then_inc(xf_summed, 1)

            def apply(p, v):
                for a in range(PAIR):
                    t = p * PAIR + a
                    pe.wait_ge(weights_ready, t + 1)
                    for c in range(GROUPS):
                        pe.wait_ge(WT_ready, freed(t * GROUPS + c))
                        for n in range(4):
                            last = nc.tensor.transpose(psT[c % 2][:, n, :], E[v][a][:, (c * 4 + n) * P:(c * 4 + n + 1) * P],
                                                       k.ident[:])
                        last.then_inc(turned, 1)
                    pe.wait_ge(WT_ready, done(t * GROUPS + GROUPS - 1))
                    pe.wait_ge(xa_copied, t + 1)
                    for j in range(NT):
                        last = nc.tensor.matmul(psA[:], WT[:, j, :], k.X[:, j, :], start=j == 0, stop=j == NT - 1)
                    last.then_inc(xa_summed, 1)

            pe.sem_inc(logits_summed, SLOTS)
            pe.sem_inc(xa_summed, 1)
            logits(0)
            with pe.Fori(0, NP // SLOTS - 1) as g:
                for v in range(SLOTS):
                    logits(g * SLOTS + v + 1)
                    neighbours(g * SLOTS + v)
                    apply(g * SLOTS + v, v)
            logits(NP - 1)
            neighbours(NP - 2)
            apply(NP - 2, 0)
            neighbours(NP - 1)
            apply(NP - 1, 1)

        @block.scalar
        def _(act):
            def exponentials(p, v):
                for a in range(PAIR):
                    t = p * PAIR + a
                    act.wait_ge(logits_summed, done(t))
                    act.wait_ge(top_ready, t + 1)
                    nc.scalar.activation(E[v][a][:], psL[:], ACT.Exp, bias=minus_top[:, DS(t, 1)],
                                         accum_out=mass[:, DS(t, 1)]).then_inc(exp_done, 1)

            def copy_out(p):
                for a in range(PAIR):
                    t = p * PAIR + a
                    act.wait_ge(xf_summed, t + 1)
                    act.wait_ge(xf_stored, 16 * t + 16)
                    nc.scalar.activation(xf_out[:], psF[:], ACT.Copy, scale=k.rscale[:, DS(t, 1)]).then_inc(xf_copied, 1)
                for a in range(PAIR):
                    t = p * PAIR + a
                    act.wait_ge(xa_summed, t + 1)
                    for c in range(GROUPS):
                        act.wait_ge(turned, t * GROUPS + c + 1)
                        nc.scalar.copy(WT[:, c * 4:(c + 1) * 4, :], psT[c % 2][:]).then_inc(WT_ready, 1)
                    act.wait_ge(xa_summed, t + 2)
                    act.wait_ge(xa_stored, 16 * t + 16)
                    nc.scalar.activation(xa_out[:], psA[:], ACT.Copy, scale=rnorm[:, DS(t, 1)]).then_inc(xa_copied, 1)

            act.sem_inc(exp_done, 1)
            act.sem_inc(xf_copied, 1)
            act.sem_inc(xa_copied, 1)
            act.sem_inc(WT_ready, SLOTS)
            exponentials(0, 0)
            with act.Fori(0, NP // SLOTS - 1) as g:
                for v in range(SLOTS):
                    exponentials(g * SLOTS + v + 1, 1 - v)
                    copy_out(g * SLOTS + v)
            exponentials(NP - 1, 1)
            copy_out(NP - 2)
            copy_out(NP - 1)

        OCTAVE_LINKS = 6
        BIT_LINKS = 7
        LAST_LINKS = 16
        PAIR_LINKS = 3 + len(OCTAVE_STEPS) * OCTAVE_LINKS + MANTISSA_STEPS * BIT_LINKS + LAST_LINKS

        @block.vector
        def _(dve):
            def largest(p):
                for a in range(PAIR):
                    t = p * PAIR + a
                    dve.wait_ge(logits_summed, done(t))
                    nc.vector.tensor_reduce(top[:, DS(t, 1)], psL[:], AX.X, ALU.max).then_inc(probed, 1)
                    dve.wait_ge(probed, t + 1)
                    nc.vector.tensor_scalar(minus_top[:, DS(t, 1)], top[:, DS(t, 1)], -1.0, None,
                                            ALU.mult).then_inc(top_ready, 1)

            def probe(ch, v):
                for a in range(PAIR):
                    ch.link(nc.vector.scalar_tensor_tensor(tie[:], E[v][a][:], mid[:, a:a + 1], E[v][a][:],
                                                           ALU.is_ge, ALU.mult, accum_out=above[:, a:a + 1]))
                ch.link(nc.vector.tensor_tensor(over, above, goal, ALU.is_ge))

            def select(p, v):
                dve.wait_ge(exp_done, p * PAIR + PAIR + 1)
                ch = Chain(dve, vec, p * PAIR_LINKS)
                ch.link(nc.vector.tensor_scalar(goal, mass[:, DS(p * PAIR, PAIR)], P_TOP, None, ALU.mult))
                ch.link(nc.vector.memset(low, LOWEST))
                for octaves in OCTAVE_STEPS:
                    ch.link(nc.vector.tensor_scalar(mid, low, 2.0 ** octaves, None, ALU.mult))
                    probe(ch, v)
                    ch.link(nc.vector.tensor_scalar(tmp, over, 2.0 ** octaves - 1.0, 1.0, ALU.mult, ALU.add))
                    ch.link(nc.vector.tensor_tensor(low, low, tmp, ALU.mult))
                ch.link(nc.vector.tensor_scalar(step, low, 0.5, None, ALU.mult), k.vector_held)
                with dve.Fori(0, MANTISSA_STEPS) as b:
                    bit = Chain(dve, vec, p * PAIR_LINKS + ch.n + b * BIT_LINKS)
                    bit.link(nc.vector.tensor_tensor(mid, low, step, ALU.add))
                    probe(bit, v)
                    bit.link(nc.vector.tensor_tensor(tmp, over, step, ALU.mult))
                    bit.link(nc.vector.tensor_tensor(low, low, tmp, ALU.add))
                    bit.link(nc.vector.tensor_scalar(step, step, 0.5, None, ALU.mult))
                    assert bit.n == BIT_LINKS
                ch = Chain(dve, vec, p * PAIR_LINKS + PAIR_LINKS - LAST_LINKS)
                for a in range(PAIR):
                    T = low[:, a:a + 1]
                    ch.link(nc.vector.tensor_scalar(tie[:], E[v][a][:], T, None, ALU.is_equal))
                    ch.link(nc.vector.tensor_tensor_scan(rank[:], tie[:], tie[:], 0.0, ALU.add, ALU.max))
                    ch.link(nc.vector.scalar_tensor_tensor(E[v][a][:], E[v][a][:], T, E[v][a][:], ALU.is_gt, ALU.mult,
                                                           accum_out=above[:, a:a + 1]))
                    ch.link(nc.vector.reciprocal(tmp[:, a:a + 1], T))
                    ch.link(nc.vector.tensor_tensor(over[:, a:a + 1], goal[:, a:a + 1], above[:, a:a + 1], ALU.subtract))
                    ch.link(nc.vector.tensor_scalar(most[:, a:a + 1], over[:, a:a + 1], tmp[:, a:a + 1], 1.0,
                                                    ALU.mult, ALU.add))
                    ch.link(nc.vector.scalar_tensor_tensor(tie[:], rank[:], most[:, a:a + 1], tie[:], ALU.is_lt, ALU.mult))
                    nc.vector.scalar_tensor_tensor(E[v][a][:], tie[:], T, E[v][a][:], ALU.mult, ALU.add,
                                                   accum_out=count[:, a:a + 1]).then_inc(vec, 1)
                    dve.wait_ge(vec, ch.base + ch.n + 1)
                    ch.n += 1
                    nc.vector.reciprocal(rnorm[:, DS(p * PAIR + a, 1)], count[:, a:a + 1]).then_inc(weights_ready, 1)
                assert ch.n == LAST_LINKS

            largest(0)
            with dve.Fori(0, NP // SLOTS - 1) as g:
                for v in range(SLOTS):
                    largest(g * SLOTS + v + 1)
                    select(g * SLOTS + v, v)
            largest(NP - 1)
            select(NP - 2, 0)
            select(NP - 1, 1)


def combine_steps(nc, k, x2, Xf, Xa, U1, U2, gamma, beta, x3):
    room = Room(nc, k.start)
    terms = [w for s in range(STEPS) for w in ((Xf[s + 1], U1[s]), (Xa[s + 1], U2[s]))]
    M = len(terms)
    w = [room.take(f"cs_w{n}", [P, FT, D], F32) for n in range(M)]
    gr = room.take("cs_gamma", [P, D], F32)
    br = room.take("cs_beta", [P, D], F32)
    x = [room.take(f"cs_x{u}", [P, D], F32) for u in range(SLOTS)]
    y = room.take("cs_y", [P, D], F32)
    xin = [room.take(f"cs_in{u}", [P, D], F32) for u in range(M)]
    xT = [room.take(f"cs_xT{u}", [P, FT, P], F32) for u in range(SLOTS)]
    stats = room.take("cs_stats", [P, 6], F32)
    mv = room.take("cs_mv", [P, 2], F32)
    sd = room.take("cs_sd", [P, 1], F32)
    rstd = room.take("cs_rstd", [P, 1], F32)
    w_in = nc.alloc_semaphore("cs_w_in")
    x_in = [nc.alloc_semaphore(f"cs_x_in{u}") for u in range(SLOTS)]
    x3_out = [nc.alloc_semaphore(f"cs_x3_out{u}") for u in range(SLOTS)]
    in_in = [nc.alloc_semaphore(f"cs_in_in{u}") for u in range(M)]
    turned = nc.alloc_semaphore("cs_turned")
    xT_ready = nc.alloc_semaphore("cs_xT_ready")
    projected = nc.alloc_semaphore("cs_projected")
    taken = nc.alloc_semaphore("cs_taken")
    var_ready = nc.alloc_semaphore("cs_var_ready")
    root_ready = nc.alloc_semaphore("cs_root_ready")
    x3_ready = nc.alloc_semaphore("cs_x3_ready")
    taken_x = nc.alloc_semaphore("cs_taken_x")
    vec = nc.alloc_semaphore("cs_vec")
    with ExitStack() as ctx:
        psT = [ctx.enter_context(nc.psum_tensor(f"cs_psT{u}", [P, FT, P], F32)) for u in range(SLOTS)]
        psY = [ctx.enter_context(nc.psum_tensor(f"cs_psY{u}", [P, D], F32)) for u in range(SLOTS)]
        block = ctx.enter_context(nc.Block())

        @block.sync
        def _(sp):
            for n, (_, u) in enumerate(terms):
                sp.dma_start(w[n][:], in_blocks(u)).then_inc(w_in, 16)
            sp.dma_start(gr[:], gamma.partition_broadcast(P)).then_inc(w_in, 16)
            sp.dma_start(br[:], beta.partition_broadcast(P)).then_inc(w_in, 16)
            for u in range(SLOTS):
                sp.dma_start(x[u][:], tile_rows(x2, u)).then_inc(x_in[u], 16)

            def load_terms(t):
                for n, (rows, _) in enumerate(terms):
                    sp.wait_ge(turned, t * M + n + 1)
                    sp.dma_start(xin[n][:], tile_rows(rows, t)).then_inc(in_in[n], 16)

            for u in range(SLOTS):
                load_terms(u)
            with sp.Fori(0, NT // SLOTS - 1) as g:
                for u in range(SLOTS):
                    load_terms((g + 1) * SLOTS + u)
                for u in range(SLOTS):
                    t = g * SLOTS + u
                    sp.wait_ge(x3_ready, t + 1)
                    sp.dma_start(tile_rows(x3, t), x[u][:]).then_inc(x3_out[u], 16)
                    sp.wait_ge(x3_out[u], g * 16 + 16)
                    sp.dma_start(x[u][:], tile_rows(x2, t + SLOTS)).then_inc(x_in[u], 16)
            for u in range(SLOTS):
                t = NT - SLOTS + u
                sp.wait_ge(x3_ready, t + 1)
                sp.dma_start(tile_rows(x3, t), x[u][:]).then_inc(x3_out[u], 16)
            for u in range(SLOTS):
                sp.wait_ge(x3_out[u], 16 * NT // SLOTS)

        @block.tensor
        def _(pe):
            pe.sem_inc(turned, M)
            pe.sem_inc(projected, SLOTS)
            pe.wait_ge(w_in, 16 * (M + 2))
            with pe.Fori(0, NT // SLOTS) as g:
                for u in range(SLOTS):
                    t = g * SLOTS + u
                    pe.wait_ge(taken, freed(t))
                    for n in range(M + 1):
                        if n < M:
                            pe.wait_ge(in_in[n], t * 16 + 16)
                            pe.wait_ge(xT_ready, freed(t * M + n))
                            transpose_tile(nc, psT[n % 2], xin[n], k.ident).then_inc(turned, 1)
                        if n:
                            pe.wait_ge(xT_ready, done(t * M + n - 1))
                            project_tile(nc, psY[u][:], xT[(n - 1) % 2], w[n - 1], n == 1, n == M).then_inc(projected, 1)

        @block.scalar
        def _(act):
            def copy_turned(t):
                for n in range(M):
                    act.wait_ge(turned, t * M + n + 1 + M)
                    act.wait_ge(projected, freed(t * M + n))
                    nc.scalar.copy(xT[n % 2][:], psT[n % 2][:]).then_inc(xT_ready, 1)

            def roots(t):
                for n in range(2):
                    act.wait_ge(var_ready, t * 2 + n + 1)
                    nc.scalar.activation(sd[:], mv[:, 1:2], ACT.Sqrt, bias=k.eps[:]).then_inc(root_ready, 1)

            act.sem_inc(xT_ready, SLOTS)
            copy_turned(0)
            with act.Fori(0, NT - 1) as t:
                copy_turned(t + 1)
                roots(t)
            roots(NT - 1)

        LINKS = 7

        @block.vector
        def _(dve):
            dve.sem_inc(taken, SLOTS)
            dve.wait_ge(w_in, 16 * (M + 2))
            with dve.Fori(0, NT // SLOTS) as g:
                for u in range(SLOTS):
                    t = g * SLOTS + u
                    ch = Chain(dve, vec, t * LINKS)
                    dve.wait_ge(x_in[u], g * 16 + 16)
                    dve.wait_ge(projected, done(t * M + M - 1))
                    nc.vector.tensor_tensor(y[:], x[u][:], psY[u][:], ALU.add).then_inc(taken, 1)
                    dve.wait_ge(taken, done(t))
                    for n in range(2):
                        ch.link(nc.vector.bn_stats(stats[:], y[:]), k.vector_held)
                        nc.vector.bn_aggr(mv[:], stats[:]).then_inc(var_ready, 1)
                        dve.wait_ge(root_ready, t * 2 + n + 1)
                        ch.link(nc.vector.reciprocal(rstd[:], sd[:]))
                        if n == 0:
                            ch.link(nc.vector.tensor_scalar(y[:], y[:], mv[:, 0:1], rstd[:], ALU.subtract, ALU.mult))
                            ch.link(nc.vector.tensor_tensor(y[:], y[:], gr[:], ALU.mult))
                            ch.link(nc.vector.tensor_tensor(y[:], y[:], br[:], ALU.add))
                            nc.vector.tensor_tensor(y[:], y[:], x[u][:], ALU.add).then_inc(taken_x, 1)
                            dve.wait_ge(taken_x, t + 1)
                        else:
                            nc.vector.tensor_scalar(x[u][:], y[:], mv[:, 0:1], rstd[:], ALU.subtract,
                                                    ALU.mult).then_inc(x3_ready, 1)
                            dve.wait_ge(x3_ready, t + 1)
                    assert ch.n == LINKS


def support(nc, k, x3, weight):
    room = Room(nc, k.upper)
    w = room.take("su_w", [P, FT, D], F32)
    x = [room.take(f"su_x{u}", [P, D], F32) for u in range(SLOTS)]
    xT = [room.take(f"su_xT{u}", [P, FT, P], F32) for u in range(SLOTS)]
    whole = room.take("su_whole", [P, D], F32)
    rest = room.take("su_rest", [P, D], F32)
    w_in = nc.alloc_semaphore("su_w_in")
    x_in = [nc.alloc_semaphore(f"su_x_in{u}") for u in range(SLOTS)]
    turned = nc.alloc_semaphore("su_turned")
    xT_ready = nc.alloc_semaphore("su_xT_ready")
    projected = nc.alloc_semaphore("su_projected")
    taken = nc.alloc_semaphore("su_taken")
    vec = nc.alloc_semaphore("su_vec")
    with ExitStack() as ctx:
        psT = [ctx.enter_context(nc.psum_tensor(f"su_psT{u}", [P, FT, P], F32)) for u in range(SLOTS)]
        psY = [ctx.enter_context(nc.psum_tensor(f"su_psY{u}", [P, D], F32)) for u in range(SLOTS)]
        block = ctx.enter_context(nc.Block())

        @block.sync
        def _(sp):
            sp.dma_start(w[:], in_blocks(weight)).then_inc(w_in, 16)
            with sp.Fori(0, NT // SLOTS) as g:
                for u in range(SLOTS):
                    t = g * SLOTS + u
                    sp.wait_ge(turned, freed(t))
                    sp.dma_start(x[u][:], tile_rows(x3, t)).then_inc(x_in[u], 16)

        @block.tensor
        def _(pe):
            pe.sem_inc(turned, SLOTS)
            pe.sem_inc(projected, SLOTS)
            pe.wait_ge(w_in, 16)
            with pe.Fori(0, NT // SLOTS) as g:
                for u in range(SLOTS):
                    t = g * SLOTS + u
                    pe.wait_ge(x_in[u], g * 16 + 16)
                    pe.wait_ge(xT_ready, freed(t))
                    transpose_tile(nc, psT[u], x[u], k.ident).then_inc(turned, 1)
                for u in range(SLOTS):
                    t = g * SLOTS + u
                    pe.wait_ge(xT_ready, done(t))
                    pe.wait_ge(taken, freed(t))
                    project_tile(nc, psY[u][:], xT[u], w).then_inc(projected, 1)

        @block.scalar
        def _(act):
            act.sem_inc(xT_ready, SLOTS)
            with act.Fori(0, NT // SLOTS) as g:
                for u in range(SLOTS):
                    t = g * SLOTS + u
                    act.wait_ge(turned, done(t))
                    act.wait_ge(projected, freed(t))
                    nc.scalar.copy(xT[u][:], psT[u][:]).then_inc(xT_ready, 1)

        LINKS = 4

        @block.vector
        def _(dve):
            dve.sem_inc(taken, SLOTS)
            with dve.Fori(0, NT // SLOTS) as g:
                for u in range(SLOTS):
                    t = g * SLOTS + u
                    dve.wait_ge(projected, done(t))
                    copied_by_vector(nc, whole[:], psY[u][:]).then_inc(taken, 1)
                    dve.wait_ge(taken, done(t))
                    split_parts(nc, Chain(dve, vec, t * LINKS), k.X3[:, t, :, :], whole[:], rest[:])


def build(nc, x, adj, adjT, L0_gnn_W_seq, L0_gnn_a1, L0_gnn_a2, L0_gnn_W_out, L0_gnn_b_out, L2_gnn_W1, L2_gnn_W2,
          L2_gnn_W3, L2_gnn_U1_0, L2_gnn_U1_1, L2_gnn_U2_0, L2_gnn_U2_1, L2_gnn_gamma, L2_gnn_beta, L3_gnn_weight,
          L3_gnn_bias, out, upto=99):
    def scratch(name, shape):
        return nc.dram_tensor(name, shape, F32, kind="Internal").ap()

    s1_rows = scratch("s1_rows", [HEADS, N])
    x1 = scratch("x1", [N, D])
    x2 = scratch("x2", [N, D])
    x3 = scratch("x3", [N, D])
    q_rows = scratch("q_rows", [DA, N])
    Xf = [x2] + [scratch(f"Xf{s + 1}", [N, D]) for s in range(STEPS)]
    Xa = [x2] + [scratch(f"Xa{s + 1}", [N, D]) for s in range(STEPS)]
    k = Kept(nc)
    gat = Gat(nc, k)
    room = Room(nc, k.upper)
    kT = room.take("kT", [DA, N], F32)
    k.after_kT = room.at
    phases = [
        lambda: prepare_adjacency(nc, k, adjT),
        lambda: attention_scores(nc, k, gat, x, L0_gnn_W_seq, L0_gnn_a1, L0_gnn_a2, s1_rows),
        lambda: lower_slope_sums(nc, k, gat),
        lambda: attention_heads(nc, k, gat, s1_rows),
        lambda: attention_output(nc, k, x, L0_gnn_W_out, L0_gnn_b_out, x1),
        lambda: normalised_sum(nc, k, adj),
        lambda: split_rows(nc, k, "sr"),
        lambda: sum_and_normalise(nc, k, "l1", x1, None, x2, True),
        lambda: logit_factors(nc, k, 0, kT, Xf[0], Xa[0], L2_gnn_W1, L2_gnn_W2, L2_gnn_W3, q_rows),
        lambda: nucleus_step(nc, k, 0, kT, q_rows, Xf[1], Xa[1]),
        lambda: logit_factors(nc, k, 1, kT, Xf[1], Xa[1], L2_gnn_W1, L2_gnn_W2, L2_gnn_W3, q_rows),
        lambda: nucleus_step(nc, k, 1, kT, q_rows, Xf[2], Xa[2]),
        lambda: combine_steps(nc, k, x2, Xf, Xa, (L2_gnn_U1_0, L2_gnn_U1_1), (L2_gnn_U2_0, L2_gnn_U2_1),
                              L2_gnn_gamma, L2_gnn_beta, x3),
        lambda: support(nc, k, x3, L3_gnn_weight),
        lambda: sum_and_normalise(nc, k, "l3", x3, L3_gnn_bias, out, False),
    ]
    for phase in phases[:upto]:
        before = nc.snapshot_sems()
        phase()
        nc.clear_and_free_semaphores(nc.allocated_since(before))
        nc.all_engine_barrier()


NAMES = ["x", "adj", "adjT", "L0_gnn_W_seq", "L0_gnn_a1", "L0_gnn_a2", "L0_gnn_W_out", "L0_gnn_b_out", "L2_gnn_W1",
         "L2_gnn_W2", "L2_gnn_W3", "L2_gnn_U1_0", "L2_gnn_U1_1", "L2_gnn_U2_0", "L2_gnn_U2_1", "L2_gnn_gamma",
         "L2_gnn_beta", "L3_gnn_weight", "L3_gnn_bias"]


def kernel(**inputs):
    import concourse.bacc as bacc
    from concourse.bass_utils import run_bass_kernel_spmd

    given = dict(inputs, adjT=np.asarray(inputs["adj"]).T)
    nc = bacc.Bacc("TRN2", target_bir_lowering=False, num_devices=1)
    arrays, args = {}, {}
    for name in NAMES:
        a = np.ascontiguousarray(given[name])
        arrays[f"in_{name}"] = a
        args[name] = nc.dram_tensor(f"in_{name}", a.shape, mybir.dt.from_np(a.dtype), kind="ExternalInput").ap()
    out = nc.dram_tensor("out_rows", (N, D), F32, kind="ExternalOutput").ap()
    build(nc, out=out, **args)
    result = run_bass_kernel_spmd(nc, [arrays], core_ids=[0])
    return result.results[0]["out_rows"]
```

```python
from contextlib import ExitStack

import numpy as np

import concourse.bass as bass
from concourse import mybir

F32 = mybir.dt.float32
F16 = mybir.dt.float16
BF16 = mybir.dt.bfloat16
ALU = mybir.AluOpType
ACT = mybir.ActivationFunctionType
AX = mybir.AxisListType
RMAX = bass.bass_isa.ReduceOp.max
DS = bass.DynSlice

P = 128
N = 2048
D = 512
NT = N // P
FT = D // P
HEADS = 16
DH = D // HEADS
DC = DH + 1
QW = 512
QT = QW // P
NQ = N // QW
DA = 64
PARTS = 3
STEPS = 2
SLOPE = 0.2
EPS = 1e-5
P_TOP = 0.9
LOWEST = 2.0 ** -15
OCTAVE_STEPS = (8, 4, 2, 1)
MANTISSA_STEPS = 23
FIRST_BITS = (1, 9)
UNROLLED_BITS = 3
PROBES_AHEAD = (1, 4)
TOP = 8
STEEP = 2.0 ** 100
SLOTS = 2


def done(t):
    return t + 1 + SLOTS


def freed(t):
    return t + 1


def hold(eng, sem, count, held):
    eng.wait_ge(sem, count)
    eng.sem_inc(held, 1)


class Chain:

    def __init__(self, eng, sem):
        self.eng, self.sem, self.n = eng, sem, 0
        eng.sem_clear(sem)

    def add(self, ins):
        self.n += 1
        ins.then_inc(self.sem, 1)

    def link(self, ins):
        self.add(ins)
        self.eng.wait_ge(self.sem, self.n)


def copied_by_vector(nc, out, src):
    return nc.vector.tensor_scalar(out, src, 1.0, None, ALU.mult)


class Room:

    def __init__(self, nc, offset):
        self.nc, self.at = nc, offset

    def take(self, name, shape, dtype):
        size = int(np.prod(shape[1:])) * mybir.dt.size(dtype)
        t = self.nc.alloc_sbuf_tensor_at(name, shape, dtype, offset=self.at)
        self.at += (size + 31) // 32 * 32
        assert self.at <= self.nc.sbuf_usable_end, (name, self.at)
        return t


class Kept:

    def __init__(self, nc):
        room = Room(nc, (nc.sbuf_base + 31) // 32 * 32)
        self.AT = room.take("AT", [P, NT, N], BF16)
        self.ident = room.take("ident", [P, P], F32)
        self.identb = room.take("identb", [P, P], BF16)
        self.eps = room.take("eps", [P, 1], F32)
        self.rscale = room.take("rscale", [P, NT], F32)
        self.dinv = room.take("dinv", [P, NT], F32)
        self.mv = room.take("mv", [P, NT, 2], F32)
        self.pool_held = nc.alloc_semaphore("pool_held")
        self.tensor_held = nc.alloc_semaphore("tensor_held")
        self.vector_held = nc.alloc_semaphore("vector_held")
        self.scalar_held = nc.alloc_semaphore("scalar_held")
        self.start = room.at
        self.X = room.take("X", [P, NT, D], F32)
        self.parts_at = room.at
        self.X3 = room.take("X3", [P, NT, PARTS, D], BF16)
        self.upper = room.at
        self.C = room.take("C", [P, NT, HEADS, DC], F32)
        self.top = room.at


def tile_rows(dram, i):
    return dram[DS(i * P, P), :]


def in_blocks(w):
    return w.rearrange("(f p) n -> p f n", p=P)


def transpose_tile(nc, out, src, ident):
    for f in range(FT):
        last = nc.tensor.transpose(out[:, f, :], src[:, f * P:(f + 1) * P], ident[:])
    return last


def project_tile(nc, out, xT, w, first=True, final=True):
    for f in range(FT):
        last = nc.tensor.matmul(out, xT[:, f, :], w[:, f, :], start=first and f == 0, stop=final and f == FT - 1)
    return last


def sum_neighbours(nc, out, AT, parts, i):
    for j in range(NT):
        for p in range(PARTS):
            last = nc.tensor.matmul(out, AT[:, j, DS(i * P, P)], parts[:, j, p, :],
                                    start=j == 0 and p == 0, stop=j == NT - 1 and p == PARTS - 1)
    return last


def prepare_adjacency(nc, k, adjT):
    room = Room(nc, k.start)
    RING = 4
    raw = [room.take(f"raw{u}", [P, N], F32) for u in range(RING)]
    row = room.take("rowsum_row", [1, N], F32)
    one = room.take("one", [1, 1], F32)
    ones = room.take("ones", [P, 1], BF16)
    colsum = room.take("colsum", [P, NT], F32)
    rowsum = room.take("rowsum", [P, NT], F32)
    deg = room.take("deg", [P, NT], F32)
    pos = room.take("pos", [P, NT], F32)
    root = room.take("root", [P, NT], F32)
    raw_in = [nc.alloc_semaphore(f"raw_in{u}") for u in range(RING)]
    cast_done = nc.alloc_semaphore("cast_done")
    ones_ready = nc.alloc_semaphore("ones_ready")
    row_summed = nc.alloc_semaphore("row_summed")
    row_ready = nc.alloc_semaphore("row_ready")
    rows_summed = nc.alloc_semaphore("rows_summed")
    deg_ready = nc.alloc_semaphore("deg_ready")
    root_ready = nc.alloc_semaphore("root_ready")
    ident_made = nc.alloc_semaphore("ident_made")
    vec = nc.alloc_semaphore("prep_vec")
    with nc.psum_tensor("ps_rowsum", [P, 512], F32) as ps, nc.psum_tensor("ps_row", [1, N], F32) as psR, \
            nc.Block() as block:

        @block.sync
        def _(sp):
            with sp.Fori(0, NT // RING) as g:
                for u in range(RING):
                    sp.wait_ge(cast_done, g * RING + u + 1)
                    sp.dma_start(raw[u][:], tile_rows(adjT, g * RING + u)).then_inc(raw_in[u], 16)

        @block.gpsimd
        def _(pool):
            nc.gpsimd.memset(k.ident[:], 0.0).then_inc(ident_made, 1)
            pool.wait_ge(ident_made, 1)
            nc.gpsimd.affine_select(out=k.ident[:], in_=k.ident[:], compare_op=ALU.not_equal, fill=1.0, base=0,
                                    pattern=[[-1, P]], channel_multiplier=1).then_inc(ident_made, 1)
            pool.wait_ge(ident_made, 2)
            nc.gpsimd.tensor_copy(k.identb[:], k.ident[:])

        @block.scalar
        def _(act):
            act.sem_inc(cast_done, RING)
            with act.Fori(0, NT // RING) as g:
                for u in range(RING):
                    t = g * RING + u
                    act.wait_ge(raw_in[u], g * 16 + 16)
                    nc.scalar.activation(k.AT[:, t, :], raw[u][:], ACT.Copy,
                                         accum_out=colsum[:, DS(t, 1)]).then_inc(cast_done, 1)
            act.wait_ge(row_summed, 1)
            nc.scalar.copy(row[:], psR[:]).then_inc(row_ready, 1)
            act.wait_ge(deg_ready, 1)
            nc.scalar.activation(root[:], deg[:], ACT.Sqrt).then_inc(root_ready, 1)

        @block.tensor
        def _(pe):
            pe.wait_ge(ones_ready, 1)

            def source(j, start, stop):
                pe.wait_ge(cast_done, j + 1 + RING)
                for c in range(NQ):
                    last = nc.tensor.matmul(psR[:, c * QW:(c + 1) * QW], ones[:], k.AT[:, j, c * QW:(c + 1) * QW],
                                            start=start, stop=stop)
                return last

            source(0, True, False)
            with pe.Fori(1, NT - 1) as j:
                source(j, False, False)
            source(NT - 1, False, True).then_inc(row_summed, 1)
            pe.wait_ge(row_ready, 1)
            for t in range(NT):
                last = nc.tensor.matmul(ps[:, t:t + 1], row[:, t * P:(t + 1) * P], one[:], start=True, stop=True)
            last.then_inc(rows_summed, 1)

        @block.vector
        def _(dve):
            ch = Chain(dve, vec)
            nc.vector.memset(k.eps[:], EPS)
            nc.vector.memset(one[:], 1.0)
            nc.vector.memset(ones[:], 1.0).then_inc(ones_ready, 1)
            dve.wait_ge(rows_summed, 1)
            ch.link(nc.vector.tensor_copy(rowsum[:], ps[:, 0:NT]))
            dve.wait_ge(cast_done, NT + RING)
            ch.link(nc.vector.tensor_scalar(pos[:], rowsum[:], 1.0, 1e-12, ALU.add, ALU.max))
            ch.link(nc.vector.reciprocal(k.rscale[:], pos[:]))
            ch.link(nc.vector.tensor_tensor(deg[:], rowsum[:], colsum[:], ALU.add))
            ch.link(nc.vector.tensor_scalar(deg[:], deg[:], 0.5, 1.0, ALU.mult, ALU.add))
            ch.link(nc.vector.tensor_scalar(pos[:], deg[:], 0.0, None, ALU.is_gt))
            nc.vector.tensor_scalar(deg[:], deg[:], 1e-30, None, ALU.max).then_inc(deg_ready, 1)
            dve.wait_ge(root_ready, 1)
            ch.link(nc.vector.reciprocal(root[:], root[:]))
            ch.link(nc.vector.tensor_tensor(k.dinv[:], root[:], pos[:], ALU.mult))


class Gat:

    def __init__(self, nc, k):
        room = Room(nc, k.start)
        self.seq = room.take("seq", [P, NT, D], F32)
        self.u = room.take("u", [P, NT, HEADS], F32)
        self.ul = room.take("ul", [P, NT, HEADS], F32)
        self.v = room.take("v", [P, NT, HEADS], F32)
        self.vl = room.take("vl", [P, NT, HEADS], F32)
        self.minus_s2 = room.take("minus_s2", [P, NT, HEADS], F32)
        self.steep_s2 = room.take("steep_s2", [P, NT, HEADS], F32)
        self.start = room.at


def attention_scores(nc, k, gat, x, W_seq, a1, a2, s1_rows):
    room = Room(nc, gat.start)
    w = room.take("w_seq", [P, FT, D], F32)
    a1r = room.take("a1r", [P, DH], F32)
    a2r = room.take("a2r", [P, DH], F32)
    xin = [room.take(f"sc_xin{u}", [P, D], F32) for u in range(SLOTS)]
    xT = [room.take(f"sc_xT{u}", [P, FT, P], F32) for u in range(SLOTS)]
    prod = [room.take(f"prod{u}", [P, D], F32) for u in range(2)]
    s1 = room.take("s1", [P, NT, HEADS], F32)
    s1_tile = [room.take(f"s1_tile{u}", [P, HEADS], F32) for u in range(SLOTS)]
    s2 = room.take("s2", [P, NT, HEADS], F32)
    s1T = room.take("s1T", [HEADS, N], F32)
    most = room.take("most", [P, HEADS], F32)
    most_all = room.take("most_all", [P, HEADS], F32)
    args = room.take("args", [P, 4, NT, HEADS], F32)
    w_in = nc.alloc_semaphore("sc_w_in")
    x_in = [nc.alloc_semaphore(f"sc_x_in{u}") for u in range(SLOTS)]
    x_turned = nc.alloc_semaphore("sc_x_turned")
    xT_ready = nc.alloc_semaphore("sc_xT_ready")
    seq_summed = nc.alloc_semaphore("sc_seq_summed")
    seq_kept = nc.alloc_semaphore("sc_seq_kept")
    s1_ready = nc.alloc_semaphore("sc_s1_ready")
    s1_turned = nc.alloc_semaphore("sc_s1_turned")
    s1T_ready = nc.alloc_semaphore("sc_s1T_ready")
    most_ready = nc.alloc_semaphore("sc_most_ready")
    most_all_ready = nc.alloc_semaphore("sc_most_all_ready")
    args_ready = nc.alloc_semaphore("sc_args_ready")
    s1_out = nc.alloc_semaphore("sc_s1_out")
    vec = nc.alloc_semaphore("sc_vec")
    with ExitStack() as ctx:
        psT = [ctx.enter_context(nc.psum_tensor(f"sc_psT{u}", [P, FT, P], F32)) for u in range(SLOTS)]
        psY = [ctx.enter_context(nc.psum_tensor(f"sc_psY{u}", [P, D], F32)) for u in range(SLOTS)]
        psS = [ctx.enter_context(nc.psum_tensor(f"sc_psS{u}", [P, 512], F32)) for u in range(SLOTS)]
        block = ctx.enter_context(nc.Block())

        @block.sync
        def _(sp):
            sp.dma_start(w[:], in_blocks(W_seq)).then_inc(w_in, 16)
            sp.dma_start(a1r[:], a1.partition_broadcast(P)).then_inc(w_in, 16)
            sp.dma_start(a2r[:], a2.partition_broadcast(P)).then_inc(w_in, 16)
            with sp.Fori(0, NT // SLOTS) as g:
                for u in range(SLOTS):
                    sp.wait_ge(x_turned, freed(g * SLOTS + u))
                    sp.dma_start(xin[u][:], tile_rows(x, g * SLOTS + u)).then_inc(x_in[u], 16)
            sp.wait_ge(s1T_ready, done(NT - 1))
            sp.dma_start(s1_rows, s1T[:]).then_inc(s1_out, 16)
            sp.wait_ge(s1_out, 16)

        @block.tensor
        def _(pe):
            pe.sem_inc(x_turned, SLOTS)
            pe.sem_inc(seq_summed, SLOTS)
            pe.sem_inc(s1_turned, SLOTS)
            pe.wait_ge(w_in, 48)
            def turn_s1(t, u):
                pe.wait_ge(s1_ready, t + 1)
                pe.wait_ge(s1T_ready, freed(t))
                nc.tensor.transpose(psS[u][0:HEADS, 0:P], s1_tile[u][:], k.ident[:]).then_inc(s1_turned, 1)

            def turn(t, u):
                pe.wait_ge(x_in[u], (t - u) * 8 + 16)
                pe.wait_ge(xT_ready, freed(t))
                transpose_tile(nc, psT[u], xin[u], k.ident).then_inc(x_turned, 1)

            def project(t, u):
                pe.wait_ge(xT_ready, done(t))
                pe.wait_ge(seq_kept, freed(t))
                project_tile(nc, psY[u][:], xT[u], w).then_inc(seq_summed, 1)

            turn(0, 0)
            turn(1, 1)
            project(0, 0)
            with pe.Fori(0, NT // SLOTS - 1) as g:
                for u in range(SLOTS):
                    t = g * SLOTS + u
                    turn(t + 2, u)
                    project(t + 1, 1 - u)
                    turn_s1(t, u)
            project(NT - 1, 1)
            turn_s1(NT - 2, 0)
            turn_s1(NT - 1, 1)

        @block.scalar
        def _(act):
            act.sem_inc(xT_ready, SLOTS)
            act.sem_inc(s1T_ready, SLOTS)

            def copy_turned(t, u):
                act.wait_ge(x_turned, done(t))
                act.wait_ge(seq_summed, freed(t))
                nc.scalar.copy(xT[u][:], psT[u][:]).then_inc(xT_ready, 1)

            def copy_s1(t, u):
                act.wait_ge(s1_turned, done(t))
                nc.scalar.copy(s1T[:, DS(t * P, P)], psS[u][0:HEADS, 0:P]).then_inc(s1T_ready, 1)

            copy_turned(0, 0)
            copy_turned(1, 1)
            with act.Fori(0, NT // SLOTS - 1) as g:
                for u in range(SLOTS):
                    copy_turned(g * SLOTS + u + 2, u)
                    copy_s1(g * SLOTS + u, u)
            copy_s1(NT - 2, 0)
            copy_s1(NT - 1, 1)
            act.wait_ge(args_ready, 1)
            for n, out in enumerate((gat.u, gat.ul, gat.v, gat.vl)):
                nc.scalar.activation(out[:], args[:, n, :, :], ACT.Exp)

        @block.gpsimd
        def _(pool):
            pool.wait_ge(most_ready, 1)
            nc.gpsimd.partition_all_reduce(most_all[:], most[:], P, RMAX).then_inc(most_all_ready, 1)


        @block.vector
        def _(dve):
            dve.sem_inc(seq_kept, SLOTS)
            dve.wait_ge(w_in, 48)
            with dve.Fori(0, NT // SLOTS) as g:
                for u in range(SLOTS):
                    t = g * SLOTS + u
                    ch = Chain(dve, vec)
                    dve.wait_ge(seq_summed, done(t))
                    copied_by_vector(nc, gat.seq[:, t, :], psY[u][:]).then_inc(seq_kept, 1)
                    dve.wait_ge(seq_kept, done(t))
                    rows = gat.seq[:, t, :].rearrange("p (h d) -> p h d", d=DH)
                    for n, a in enumerate((a1r, a2r)):
                        heads = prod[n][:].rearrange("p (h d) -> p h d", d=DH)
                        ch.link(nc.vector.tensor_tensor(heads, rows, a[:].unsqueeze(1).broadcast_to([P, HEADS, DH]),
                                                        ALU.mult))
                        if n == 0:
                            dve.wait_ge(s1_turned, freed(t))
                            nc.vector.tensor_reduce(s1_tile[u][:], heads, AX.X, ALU.add).then_inc(s1_ready, 1)
                            dve.wait_ge(s1_ready, t + 1)
                            ch.link(copied_by_vector(nc, s1[:, t, :], s1_tile[u][:]))
                        else:
                            ch.link(nc.vector.tensor_reduce(s2[:, t, :], heads, AX.X, ALU.add))
            dve.wait_ge(s1_ready, NT)
            ch = Chain(dve, vec)
            nc.vector.tensor_reduce(most[:], s2[:].rearrange("p t h -> p h t"), AX.X, ALU.max).then_inc(most_ready, 1)
            nc.vector.tensor_scalar(gat.minus_s2[:], s2[:], -1.0, None, ALU.mult)
            nc.vector.tensor_scalar(gat.steep_s2[:], s2[:], STEEP, None, ALU.mult)
            dve.wait_ge(most_all_ready, 1)
            across = most_all[:].unsqueeze(1).broadcast_to([P, NT, HEADS])
            ch.link(nc.vector.tensor_tensor(s1[:], s1[:], across, ALU.add))
            ch.link(nc.vector.tensor_tensor(s2[:], s2[:], across, ALU.subtract))
            ch.link(nc.vector.tensor_scalar(args[:, 0, :, :], s1[:], 1.0 - SLOPE, 0.0, ALU.mult, ALU.min))
            ch.link(nc.vector.tensor_scalar(args[:, 1, :, :], s1[:], SLOPE - 1.0, 0.0, ALU.mult, ALU.min))
            ch.link(copied_by_vector(nc, args[:, 2, :, :], s2[:]))
            nc.vector.tensor_scalar(args[:, 3, :, :], s2[:], SLOPE, None, ALU.mult).then_inc(args_ready, 1)


def lower_slope_sums(nc, k, gat):
    AT_ONCE = 4
    HC = HEADS * DC // 2
    room = Room(nc, gat.start)
    V3 = [room.take(f"lo_V3_{n}", [P, NT, 2, HC], BF16) for n in range(2)]
    assert room.at <= k.upper, (room.at, k.upper)
    room = Room(nc, k.top)
    V3.append(room.take("lo_V3_2", [P, NT, 2, HC], BF16))
    whole = [room.take(f"lo_whole{u}", [P, HEADS, DC], F32) for u in range(SLOTS)]
    rest = room.take("lo_rest", [P, HEADS * DC], F32)
    weighed = nc.alloc_semaphore("lo_weighed")
    split = nc.alloc_semaphore("lo_split")
    summed = nc.alloc_semaphore("lo_summed")
    kept = nc.alloc_semaphore("lo_kept")
    vec = nc.alloc_semaphore("lo_vec")
    with ExitStack() as ctx:
        ps = [ctx.enter_context(nc.psum_tensor(f"lo_ps{n}", [P, 2, 512], F32)) for n in range(AT_ONCE)]
        block = ctx.enter_context(nc.Block())

        @block.gpsimd
        def _(pool):
            with pool.Fori(0, NT // SLOTS) as g:
                for u in range(SLOTS):
                    t = g * SLOTS + u
                    hold(pool, split, freed(t), k.pool_held)
                    weight = gat.vl[:, DS(t, 1), :].rearrange("p a h -> p (a h)").unsqueeze(2)
                    rows = gat.seq[:, DS(t, 1), :].rearrange("p a (h d) -> p (a h) d", d=DH)
                    nc.gpsimd.tensor_tensor(whole[u][:, :, 0:DH], rows, weight.broadcast_to([P, HEADS, DH]),
                                            ALU.mult).then_inc(weighed, 1)
                    nc.gpsimd.tensor_copy(whole[u][:, :, DH:DC], weight).then_inc(weighed, 1)

        @block.vector
        def _(dve):
            dve.sem_inc(split, SLOTS)
            with dve.Fori(0, NT // SLOTS) as g:
                for u in range(SLOTS):
                    t = g * SLOTS + u
                    ch = Chain(dve, vec)
                    parts = [v[:, t, :, :].rearrange("p c n -> p (c n)") for v in V3]
                    rows = whole[u][:].rearrange("p h d -> p (h d)")
                    dve.wait_ge(weighed, t * 2 + 2)
                    ch.link(copied_by_vector(nc, parts[0], rows))
                    ch.link(nc.vector.tensor_tensor(rest[:], rows, parts[0], ALU.subtract))
                    ch.link(copied_by_vector(nc, parts[1], rest[:]))
                    nc.vector.tensor_tensor(parts[2], rest[:], parts[1], ALU.subtract).then_inc(split, 1)
                    hold(dve, split, done(t), k.vector_held)

        @block.tensor
        def _(pe):
            def source(out, i, j, start, stop):
                for p in range(PARTS):
                    for c in range(2):
                        last = nc.tensor.matmul(out[:, c, 0:HC], k.AT[:, j, DS(i * P, P)], V3[p][:, j, c, :],
                                                start=start and p == 0, stop=stop and p == PARTS - 1)
                return last

            def first_tiles(j, start, stop):
                pe.wait_ge(split, done(j))
                for i in range(AT_ONCE):
                    last = source(ps[i], i, j, start, stop)
                return last

            first_tiles(0, True, False)
            with pe.Fori(1, NT - 1) as j:
                first_tiles(j, False, False)
            first_tiles(NT - 1, False, True).then_inc(summed, AT_ONCE)
            with pe.Fori(1, NT // AT_ONCE) as g:
                for n in range(AT_ONCE):
                    i = g * AT_ONCE + n
                    pe.wait_ge(kept, i - AT_ONCE + 1)
                    for j in range(NT):
                        last = source(ps[n], i, j, j == 0, j == NT - 1)
                    last.then_inc(summed, 1)

        @block.scalar
        def _(act):
            with act.Fori(0, NT // AT_ONCE) as g:
                for n in range(AT_ONCE):
                    i = g * AT_ONCE + n
                    act.wait_ge(summed, i + 1)
                    nc.scalar.copy(k.C[:, i, :, :].rearrange("p (c h) d -> p c (h d)", c=2),
                                   ps[n][:, :, 0:HC]).then_inc(kept, 1)


def attention_heads(nc, k, gat, s1_rows):
    BY_SIGMOID = 9
    BOTH = 2 * DC
    room = Room(nc, gat.start)
    B = [room.take(f"B{u}", [P, NT, QW], BF16) for u in range(SLOTS)]
    V3 = [room.take("hd_V3_0", [P, NT, PARTS * BOTH], BF16)]
    assert room.at <= k.upper, (room.at, k.upper)
    room = Room(nc, k.top)
    V3.append(room.take("hd_V3_1", [P, NT, PARTS * BOTH], BF16))
    s1b = [room.take(f"s1b{q}", [P, QW], F32) for q in range(2)]
    whole = room.take("hd_whole", [P, NT, BOTH], F32)
    raw = [room.take(f"hd_raw{u}", [P, QT, PARTS, BOTH], F32) for u in range(SLOTS)]
    sums = room.take("hd_sums", [P, QT, BOTH], F32)
    s1_in = [nc.alloc_semaphore(f"hd_s1_in{u}") for u in range(SLOTS)]
    masked = nc.alloc_semaphore("hd_masked")
    compared = nc.alloc_semaphore("hd_compared")
    summed = nc.alloc_semaphore("hd_summed")
    copied = nc.alloc_semaphore("hd_copied")
    added = nc.alloc_semaphore("hd_added")
    v_split = nc.alloc_semaphore("hd_v_split")
    pool_steps = nc.alloc_semaphore("hd_pool_steps")
    with ExitStack() as ctx:
        ps = [ctx.enter_context(nc.psum_tensor(f"hd_ps{u}", [P, 2, 512], F32)) for u in range(SLOTS)]
        block = ctx.enter_context(nc.Block())

        @block.sync
        def _(sp):
            with sp.Fori(0, HEADS) as h:
                for q in range(NQ):
                    sp.wait_ge(masked, freed(h * NQ + q))
                    sp.dma_start(s1b[q % 2][:], s1_rows[h, q * QW:(q + 1) * QW].partition_broadcast(P)
                                 ).then_inc(s1_in[q % 2], 16)

        @block.vector
        def _(dve):
            dve.sem_inc(masked, SLOTS)
            with dve.Fori(0, HEADS) as h:
                for q in range(NQ):
                    dve.wait_ge(s1_in[q % 2], h * (16 * NQ // 2) + 16 * (q // 2 + 1))
                    dve.wait_ge(summed, freed(h * NQ + q))
                    for j in range(BY_SIGMOID, NT):
                        nc.vector.scalar_tensor_tensor(
                            B[q % 2][:, j, :], s1b[q % 2][:], gat.minus_s2[:, j, DS(h, 1)],
                            k.AT[:, j, q * QW:(q + 1) * QW], ALU.is_ge, ALU.mult)
                    dve.wait_ge(compared, h * NQ + q + 1)
                    compared_block = B[q % 2][:, 0:BY_SIGMOID, :]
                    nc.vector.tensor_tensor(compared_block, compared_block,
                                            k.AT[:, 0:BY_SIGMOID, q * QW:(q + 1) * QW], ALU.mult).then_inc(masked, 1)

        @block.tensor
        def _(pe):
            pe.sem_inc(summed, SLOTS)
            with pe.Fori(0, HEADS // 2) as g:
                for v in range(2):
                    h = g * 2 + v
                    pe.wait_ge(v_split, h + 1)
                    for q in range(NQ):
                        pe.wait_ge(masked, done(h * NQ + q))
                        pe.wait_ge(copied, freed(h * NQ + q))
                        for i in range(QT):
                            for j in range(NT):
                                last = nc.tensor.matmul(
                                    ps[q % 2][:, i // 2, (i % 2) * PARTS * BOTH:(i % 2 + 1) * PARTS * BOTH],
                                    B[q % 2][:, j, i * P:(i + 1) * P], V3[v][:, j, :], start=j == 0, stop=j == NT - 1)
                        last.then_inc(summed, 1)

        @block.scalar
        def _(act):
            def compare(h, q):
                act.wait_ge(s1_in[q % 2], h * (16 * NQ // 2) + 16 * (q // 2 + 1))
                hold(act, summed, freed(h * NQ + q), k.scalar_held)
                for j in range(BY_SIGMOID):
                    last = nc.scalar.activation(B[q % 2][:, j, :], s1b[q % 2][:], ACT.Sigmoid,
                                                bias=gat.steep_s2[:, j, DS(h, 1)], scale=STEEP)
                last.then_inc(compared, 1)

            def copy_sums(h, q):
                Q = h * NQ + q
                act.wait_ge(summed, done(Q))
                act.wait_ge(added, freed(Q))
                nc.scalar.copy(raw[q % 2][:].rearrange("p (b i) a c -> p b (i a c)", b=2),
                               ps[q % 2][:, :, 0:2 * PARTS * BOTH]).then_inc(copied, 1)

            def head(h, before):
                for q in range(NQ):
                    compare(h, q)
                    if q >= SLOTS:
                        copy_sums(h, q - SLOTS)
                    elif before is not None:
                        copy_sums(before, NQ - SLOTS + q)

            act.sem_inc(copied, SLOTS)
            head(0, None)
            with act.Fori(0, HEADS - 1) as g:
                head(g + 1, g)
            for q in range(NQ - SLOTS, NQ):
                copy_sums(HEADS - 1, q)


        @block.gpsimd
        def _(pool):
            def split_v(h, v):
                ch = Chain(pool, pool_steps)
                rows = gat.seq[:, :, DS(h * DH, DH)]
                for n, weights in enumerate((gat.v, gat.vl)):
                    weight = weights[:, :, DS(h, 1)]
                    ch.link(nc.gpsimd.tensor_tensor(whole[:, :, n * DC:n * DC + DH], rows,
                                                    weight.broadcast_to([P, NT, DH]), ALU.mult))
                    ch.link(nc.gpsimd.tensor_copy(whole[:, :, n * DC + DH:(n + 1) * DC], weight))
                parts = [V3[v][:, :, a * BOTH:(a + 1) * BOTH] for a in range(PARTS)]
                ch.link(nc.gpsimd.tensor_copy(parts[0], whole[:]))
                ch.link(nc.gpsimd.tensor_tensor(whole[:], whole[:], parts[0], ALU.subtract))
                ch.link(nc.gpsimd.tensor_copy(parts[1], whole[:]))
                nc.gpsimd.tensor_tensor(parts[2], whole[:], parts[1], ALU.subtract).then_inc(v_split, 1)
                hold(pool, v_split, h + 1, k.pool_held)

            def combine(h):
                ch = Chain(pool, pool_steps)
                for q in range(NQ):
                    Q = h * NQ + q
                    hold(pool, copied, done(Q), k.pool_held)
                    ch.link(nc.gpsimd.tensor_tensor(sums[:], raw[q % 2][:, :, 0, :], raw[q % 2][:, :, 1, :], ALU.add))
                    nc.gpsimd.tensor_tensor(sums[:], sums[:], raw[q % 2][:, :, 2, :], ALU.add).then_inc(added, 1)
                    hold(pool, added, done(Q), k.pool_held)
                    tiles = slice(q * QT, (q + 1) * QT)
                    C = k.C[:, tiles, h, :]
                    up, low = sums[:, :, 0:DC], sums[:, :, DC:BOTH]
                    u = gat.u[:, tiles, DS(h, 1)].broadcast_to([P, QT, DC])
                    ul = gat.ul[:, tiles, DS(h, 1)].broadcast_to([P, QT, DC])
                    ch.link(nc.gpsimd.tensor_tensor(low, C, low, ALU.subtract))
                    ch.link(nc.gpsimd.tensor_tensor(low, low, ul, ALU.mult))
                    ch.link(nc.gpsimd.tensor_tensor(up, up, u, ALU.mult))
                    ch.link(nc.gpsimd.tensor_tensor(C, up, low, ALU.add))

            pool.sem_inc(added, SLOTS)
            split_v(0, 0)
            split_v(1, 1)
            with pool.Fori(0, HEADS // 2 - 1) as g:
                for v in range(2):
                    h = g * 2 + v
                    combine(h)
                    split_v(h + 2, v)
            for h in (HEADS - 2, HEADS - 1):
                combine(h)


def attention_output(nc, k, x, W_out, b_out):
    room = Room(nc, k.parts_at)
    w = room.take("w_out", [P, FT, D], F32)
    bias = room.take("ao_bias", [P, D], F32)
    xin = [room.take(f"ao_x{u}", [P, D], F32) for u in range(SLOTS)]
    hid = [room.take(f"ao_hid{u}", [P, D], F32) for u in range(SLOTS)]
    hT = [room.take(f"ao_hT{u}", [P, FT, P], F32) for u in range(SLOTS)]
    rden = [room.take(f"ao_rden{u}", [P, HEADS], F32) for u in range(SLOTS)]
    whole = [room.take(f"ao_whole{u}", [P, D], F32) for u in range(SLOTS)]
    low = [room.take(f"ao_low{u}", [P, D], F32) for u in range(SLOTS)]
    stats = room.take("ao_stats", [P, 6], F32)
    mv = room.take("ao_mv", [P, 2], F32)
    w_in = nc.alloc_semaphore("ao_w_in")
    x_in = [nc.alloc_semaphore(f"ao_x_in{u}") for u in range(SLOTS)]
    hid_ready = nc.alloc_semaphore("ao_hid_ready")
    turned = nc.alloc_semaphore("ao_turned")
    hT_ready = nc.alloc_semaphore("ao_hT_ready")
    summed = nc.alloc_semaphore("ao_summed")
    low_ready = nc.alloc_semaphore("ao_low_ready")
    exp_done = nc.alloc_semaphore("ao_exp_done")
    rows_ready = nc.alloc_semaphore("ao_rows_ready")
    vec = nc.alloc_semaphore("ao_vec")
    with ExitStack() as ctx:
        psT = [ctx.enter_context(nc.psum_tensor(f"ao_psT{u}", [P, FT, P], F32)) for u in range(SLOTS)]
        psY = [ctx.enter_context(nc.psum_tensor(f"ao_psY{u}", [P, D], F32)) for u in range(SLOTS)]
        block = ctx.enter_context(nc.Block())

        @block.sync
        def _(sp):
            sp.dma_start(w[:], in_blocks(W_out)).then_inc(w_in, 16)
            sp.dma_start(bias[:], b_out.partition_broadcast(P)).then_inc(w_in, 16)
            with sp.Fori(0, NT // SLOTS) as g:
                for u in range(SLOTS):
                    t = g * SLOTS + u
                    sp.wait_ge(rows_ready, freed(t))
                    sp.dma_start(xin[u][:], tile_rows(x, t)).then_inc(x_in[u], 16)

        @block.tensor
        def _(pe):
            def turn(t, u):
                pe.wait_ge(hid_ready, t + 1)
                pe.wait_ge(hT_ready, freed(t))
                transpose_tile(nc, psT[u], hid[u], k.ident).then_inc(turned, 1)

            def project(t, u):
                pe.wait_ge(hT_ready, done(t))
                pe.wait_ge(low_ready, freed(t))
                project_tile(nc, psY[u][:], hT[u], w).then_inc(summed, 1)

            pe.sem_inc(turned, SLOTS)
            pe.sem_inc(summed, SLOTS)
            pe.wait_ge(w_in, 32)
            turn(0, 0)
            with pe.Fori(0, NT // SLOTS - 1) as g:
                for u in range(SLOTS):
                    turn(g * SLOTS + u + 1, 1 - u)
                    project(g * SLOTS + u, u)
            turn(NT - 1, 1)
            project(NT - 2, 0)
            project(NT - 1, 1)

        @block.scalar
        def _(act):
            def copy_turned(t, u):
                act.wait_ge(turned, done(t))
                act.wait_ge(summed, freed(t))
                nc.scalar.copy(hT[u][:], psT[u][:]).then_inc(hT_ready, 1)

            def exponential(t, u):
                act.wait_ge(low_ready, done(t))
                nc.scalar.activation(low[u][:], low[u][:], ACT.Exp).then_inc(exp_done, 1)

            act.sem_inc(hT_ready, SLOTS)
            copy_turned(0, 0)
            with act.Fori(0, NT // SLOTS - 1) as g:
                for u in range(SLOTS):
                    copy_turned(g * SLOTS + u + 1, 1 - u)
                    exponential(g * SLOTS + u, u)
            copy_turned(NT - 1, 1)
            exponential(NT - 2, 0)
            exponential(NT - 1, 1)

        @block.vector
        def _(dve):
            def divide(t, u):
                ch = Chain(dve, vec)
                dve.wait_ge(turned, freed(t))
                ch.link(nc.vector.reciprocal(rden[u][:].unsqueeze(2), k.C[:, t, :, DH:DC]))
                nc.vector.tensor_tensor(hid[u][:].rearrange("p (h d) -> p h d", d=DH), k.C[:, t, :, 0:DH],
                                        rden[u][:].unsqueeze(2).broadcast_to([P, HEADS, DH]),
                                        ALU.mult).then_inc(hid_ready, 1)

            def negative_part(t, u):
                ch = Chain(dve, vec)
                dve.wait_ge(summed, done(t))
                ch.link(nc.vector.tensor_tensor(whole[u][:], psY[u][:], bias[:], ALU.add))
                nc.vector.tensor_scalar(low[u][:], whole[u][:], 0.0, None, ALU.min).then_inc(low_ready, 1)

            def add_up(t, u):
                ch = Chain(dve, vec)
                dve.wait_ge(x_in[u], (t - u) * 8 + 16)
                ch.link(nc.vector.scalar_tensor_tensor(whole[u][:], whole[u][:], 0.0, xin[u][:], ALU.max, ALU.add))
                dve.wait_ge(exp_done, t + 1)
                ch.link(nc.vector.scalar_tensor_tensor(k.X[:, t, :], low[u][:], -1.0, whole[u][:], ALU.add, ALU.add))
                dve.sem_inc(rows_ready, 1)
                ch.link(nc.vector.bn_stats(stats[:], k.X[:, t, :]))
                ch.link(nc.vector.bn_aggr(mv[:], stats[:]))
                ch.link(copied_by_vector(nc, k.mv[:, t, :], mv[:]))

            dve.sem_inc(low_ready, SLOTS)
            dve.sem_inc(rows_ready, SLOTS)
            dve.wait_ge(w_in, 32)
            def step(t, u, ahead=True):
                if ahead:
                    divide(t + 3, 1 - u)
                negative_part(t + 1, 1 - u)
                add_up(t, u)

            for t in range(3):
                divide(t, t % 2)
            negative_part(0, 0)
            with dve.Fori(0, NT // SLOTS - 2) as g:
                for u in range(SLOTS):
                    step(g * SLOTS + u, u)
            step(NT - 4, 0)
            step(NT - 3, 1, False)
            step(NT - 2, 0, False)
            add_up(NT - 1, 1)


def sources_outside(nc, pe, ready, outs, stationary, parts):
    def source(j, start, stop):
        for sem, count in ready(j):
            pe.wait_ge(sem, count)
        for n, out in enumerate(outs):
            for p in range(PARTS):
                last = nc.tensor.matmul(out, stationary(j, n), parts[:, j, p, :], start=start and p == 0,
                                        stop=stop and p == PARTS - 1)
        return last

    source(0, True, False)
    with pe.Fori(1, NT - 1) as j:
        source(j, False, False)
    return source(NT - 1, False, True)


def normalised_sum(nc, k, adj, x1):
    QUARTERS = NT // QT
    RING = 3
    RAWS = 4
    room = Room(nc, k.upper)
    S = [room.take(f"S{r}", [P, NT, QW], BF16) for r in range(RING)]
    raw = [room.take(f"ns_raw{u}", [P, QW], F32) for u in range(RAWS)]
    rows = [room.take(f"ns_rows{u}", [P, D], F32) for u in range(SLOTS)]
    tmp = room.take("ns_tmp", [P, D], F32)
    sd = room.take("ns_sd", [P, NT], F32)
    rstd = room.take("ns_rstd", [P, NT], F32)
    offset = room.take("ns_offset", [P, NT], F32)
    rstd_dinv = room.take("ns_rstd_dinv", [P, NT], F32)
    offset_dinv = room.take("ns_offset_dinv", [P, NT], F32)
    raw_in = [nc.alloc_semaphore(f"ns_raw_in{u}") for u in range(RAWS)]
    made = nc.alloc_semaphore("ns_made")
    root_ready = nc.alloc_semaphore("ns_root_ready")
    rstd_ready = nc.alloc_semaphore("ns_rstd_ready")
    x1_ready = nc.alloc_semaphore("ns_x1_ready")
    rounded = nc.alloc_semaphore("ns_rounded")
    scaled = nc.alloc_semaphore("ns_scaled")
    x1_out = [nc.alloc_semaphore(f"ns_x1_out{u}") for u in range(SLOTS)]
    split = nc.alloc_semaphore("ns_split")
    summed = nc.alloc_semaphore("ns_summed")
    kept = nc.alloc_semaphore("ns_kept")
    vec = nc.alloc_semaphore("ns_vec")
    with ExitStack() as ctx:
        psG = ctx.enter_context(nc.psum_tensor("ns_psG", [P, QT, D], F32))
        ps = [ctx.enter_context(nc.psum_tensor(f"ns_ps{u}", [P, D], F32)) for u in range(SLOTS)]
        block = ctx.enter_context(nc.Block())

        @block.sync
        def _(sp):
            for q in range(QUARTERS):
                with sp.Fori(0, NT // RAWS) as g:
                    for u in range(RAWS):
                        t = g * RAWS + u
                        sp.wait_ge(made, t + q * NT + 1)
                        sp.dma_start(raw[u][:], adj[DS(t * P, P), q * QW:(q + 1) * QW]).then_inc(raw_in[u], 16)

        @block.gpsimd
        def _(pool):
            pool.sem_inc(made, RAWS)
            for q in range(QUARTERS):
                if q >= RING:
                    pool.wait_ge(summed, (q - RING + 1) * QT)
                with pool.Fori(0, NT // RAWS) as g:
                    for u in range(RAWS):
                        t = g * RAWS + u
                        hold(pool, raw_in[u], g * 16 + 16 + q * (16 // RAWS) * NT, k.pool_held)
                        nc.gpsimd.tensor_tensor(S[q % RING][:, t, :], raw[u][:], k.AT[:, t, q * QW:(q + 1) * QW],
                                                ALU.add).then_inc(made, 1)

        @block.tensor
        def _(pe):
            last = sources_outside(nc, pe, lambda j: ((made, j + 1 + RAWS), (split, j + 1)),
                                   [psG[:, n, :] for n in range(QT)],
                                   lambda j, n: S[0][:, j, n * P:(n + 1) * P], k.X3)
            last.then_inc(summed, QT)
            for q in range(1, QUARTERS):
                pe.wait_ge(made, (q + 1) * NT + RAWS)
                with pe.Fori(0, QT // SLOTS) as g:
                    for u in range(SLOTS):
                        t = g * SLOTS + u
                        pe.wait_ge(kept, freed(t + (q - 1) * QT))
                        sum_neighbours(nc, ps[u][:], S[q % RING], k.X3, t).then_inc(summed, 1)

        @block.scalar
        def _(act):
            nc.scalar.activation(sd[:], k.mv[:, :, 1], ACT.Sqrt, bias=k.eps[:]).then_inc(root_ready, 1)
            act.wait_ge(rstd_ready, 1)
            with act.Fori(0, NT // SLOTS) as g:
                for u in range(SLOTS):
                    t = g * SLOTS + u
                    hold(act, x1_out[u], g * 16 + 16, k.scalar_held)
                    nc.scalar.activation(rows[u][:], k.X[:, t, :], ACT.Identity, bias=offset[:, DS(t, 1)],
                                         scale=rstd[:, DS(t, 1)]).then_inc(x1_ready, 1)
                    act.wait_ge(x1_ready, t + 1)
                    act.dma_start(tile_rows(x1, t), rows[u][:]).then_inc(x1_out[u], 16)
                    nc.scalar.activation(k.X[:, t, :], k.X[:, t, :], ACT.Identity, bias=offset_dinv[:, DS(t, 1)],
                                         scale=rstd_dinv[:, DS(t, 1)]).then_inc(scaled, 1)
                    hold(act, scaled, t + 1, k.scalar_held)
                    nc.scalar.copy(k.X3[:, t, 0, :], k.X[:, t, :]).then_inc(rounded, 1)
            for u in range(SLOTS):
                act.wait_ge(x1_out[u], 16 * (NT // SLOTS + 1))

        @block.vector
        def _(dve):
            dve.sem_inc(kept, SLOTS)
            for u in range(SLOTS):
                dve.sem_inc(x1_out[u], 16)
            ch = Chain(dve, vec)
            dve.wait_ge(root_ready, 1)
            ch.link(nc.vector.reciprocal(rstd[:], sd[:]))
            ch.link(nc.vector.tensor_tensor(offset[:], k.mv[:, :, 0], rstd[:], ALU.mult))
            ch.link(nc.vector.tensor_scalar(offset[:], offset[:], -1.0, None, ALU.mult))
            ch.link(nc.vector.tensor_tensor(rstd_dinv[:], rstd[:], k.dinv[:], ALU.mult))
            nc.vector.tensor_tensor(offset_dinv[:], offset[:], k.dinv[:], ALU.mult).then_inc(rstd_ready, 1)
            dve.wait_ge(rstd_ready, 1)
            with dve.Fori(0, NT) as t:
                ch = Chain(dve, vec)
                dve.wait_ge(rounded, t + 1)
                parts = k.X3[:, t, :, :]
                ch.link(nc.vector.tensor_tensor(tmp[:], k.X[:, t, :], parts[:, 0, :], ALU.subtract))
                ch.link(copied_by_vector(nc, parts[:, 1, :], tmp[:]))
                nc.vector.tensor_tensor(parts[:, 2, :], tmp[:], parts[:, 1, :], ALU.subtract).then_inc(split, 1)
                hold(dve, split, t + 1, k.vector_held)

            def keep(t, sum_of_tile, count):
                ch = Chain(dve, vec)
                dve.wait_ge(summed, count)
                ch.link(nc.vector.scalar_tensor_tensor(tmp[:], sum_of_tile, 0.5, k.X[:, t, :], ALU.mult, ALU.add))
                return nc.vector.tensor_scalar(k.X[:, t, :], tmp[:], k.dinv[:, DS(t, 1)], None, ALU.mult)

            for t in range(QT):
                ch = Chain(dve, vec)
                keep(t, psG[:, t, :], QT).then_inc(vec, 1)
                dve.wait_ge(vec, 2)
            with dve.Fori(0, (NT - QT) // SLOTS) as g:
                for u in range(SLOTS):
                    t = g * SLOTS + u
                    keep(t + QT, ps[u][:], t + QT + 1).then_inc(kept, 1)
                    hold(dve, kept, done(t), k.vector_held)


def sum_and_normalise(nc, k, name, base, bias_row, out, keep):
    AT_ONCE = RING = 4
    room = Room(nc, k.upper)
    rows = [room.take(f"{name}_rows{u}", [P, D], F32) for u in range(RING)]
    bias = room.take(f"{name}_bias", [P, D], F32)
    rest = room.take(f"{name}_rest", [P, D], F32)
    stats = room.take(f"{name}_stats", [P, 6], F32)
    mv = room.take(f"{name}_mv", [P, 2], F32)
    sd = room.take(f"{name}_sd", [P, 1], F32)
    rstd = room.take(f"{name}_rstd", [P, 1], F32)
    bias_in = nc.alloc_semaphore(f"{name}_bias_in")
    rows_in = [nc.alloc_semaphore(f"{name}_rows_in{u}") for u in range(RING)]
    rows_out = [nc.alloc_semaphore(f"{name}_rows_out{u}") for u in range(RING)]
    rounded = nc.alloc_semaphore(f"{name}_rounded")
    split = nc.alloc_semaphore(f"{name}_split")
    summed = nc.alloc_semaphore(f"{name}_summed")
    added = nc.alloc_semaphore(f"{name}_added")
    var_ready = nc.alloc_semaphore(f"{name}_var_ready")
    root_ready = nc.alloc_semaphore(f"{name}_root_ready")
    out_ready = nc.alloc_semaphore(f"{name}_out_ready")
    vec = nc.alloc_semaphore(f"{name}_vec")
    with ExitStack() as ctx:
        psG = ctx.enter_context(nc.psum_tensor(f"{name}_psG", [P, AT_ONCE, D], F32))
        ps = [ctx.enter_context(nc.psum_tensor(f"{name}_ps{u}", [P, D], F32)) for u in range(RING)]
        block = ctx.enter_context(nc.Block())

        @block.sync
        def _(sp):
            if bias_row is not None:
                sp.dma_start(bias[:], bias_row.partition_broadcast(P)).then_inc(bias_in, 16)
            for u in range(RING):
                sp.dma_start(rows[u][:], tile_rows(base, u)).then_inc(rows_in[u], 16)
            with sp.Fori(0, NT // RING - 1) as g:
                for u in range(RING):
                    t = g * RING + u
                    sp.wait_ge(out_ready, t + 1)
                    sp.dma_start(tile_rows(out, t), rows[u][:]).then_inc(rows_out[u], 16)
                    sp.wait_ge(rows_out[u], g * 16 + 16)
                    sp.dma_start(rows[u][:], tile_rows(base, t + RING)).then_inc(rows_in[u], 16)
            for u in range(RING):
                t = NT - RING + u
                sp.wait_ge(out_ready, t + 1)
                sp.dma_start(tile_rows(out, t), rows[u][:]).then_inc(rows_out[u], 16)
            for u in range(RING):
                sp.wait_ge(rows_out[u], 16 * NT // RING)

        @block.tensor
        def _(pe):
            last = sources_outside(nc, pe, lambda j: ((split, j + 1),), [psG[:, n, :] for n in range(AT_ONCE)],
                                   lambda j, n: k.AT[:, j, n * P:(n + 1) * P], k.X3)
            last.then_inc(summed, AT_ONCE)
            for u in range(RING):
                sum_neighbours(nc, ps[u][:], k.AT, k.X3, AT_ONCE + u).then_inc(summed, 1)
            with pe.Fori(2, NT // RING) as g:
                for u in range(RING):
                    t = g * RING + u
                    pe.wait_ge(added, t - RING + 1)
                    sum_neighbours(nc, ps[u][:], k.AT, k.X3, t).then_inc(summed, 1)

        @block.scalar
        def _(act):
            with act.Fori(0, NT) as j:
                nc.scalar.copy(k.X3[:, j, 0, :], k.X[:, j, :]).then_inc(rounded, 1)
            with act.Fori(0, NT) as t:
                act.wait_ge(var_ready, t + 1)
                nc.scalar.activation(sd[:], mv[:, 1:2], ACT.Sqrt, bias=k.eps[:]).then_inc(root_ready, 1)

        @block.vector
        def _(dve):
            def finish(t, u, sum_of_tile):
                ch = Chain(dve, vec)
                dve.wait_ge(rows_in[u], (t - u) * (16 // RING) + 16)
                if bias_row is not None:
                    ch.link(nc.vector.tensor_tensor(rows[u][:], rows[u][:], bias[:], ALU.add))
                dve.wait_ge(summed, t + 1)
                nc.vector.tensor_tensor(rows[u][:], rows[u][:], sum_of_tile, ALU.add).then_inc(added, 1)
                dve.wait_ge(added, t + 1)
                ch.link(nc.vector.bn_stats(stats[:], rows[u][:]))
                nc.vector.bn_aggr(mv[:], stats[:]).then_inc(var_ready, 1)
                dve.wait_ge(root_ready, t + 1)
                ch.link(nc.vector.reciprocal(rstd[:], sd[:]))
                normal = nc.vector.tensor_scalar(rows[u][:], rows[u][:], mv[:, 0:1], rstd[:], ALU.subtract, ALU.mult)
                if keep:
                    ch.link(normal)
                    normal = copied_by_vector(nc, k.X[:, t, :], rows[u][:])
                normal.then_inc(out_ready, 1)

            with dve.Fori(0, NT) as j:
                ch = Chain(dve, vec)
                parts = k.X3[:, j, :, :]
                dve.wait_ge(rounded, j + 1)
                ch.link(nc.vector.tensor_tensor(rest[:], k.X[:, j, :], parts[:, 0, :], ALU.subtract))
                ch.link(copied_by_vector(nc, parts[:, 1, :], rest[:]))
                nc.vector.tensor_tensor(parts[:, 2, :], rest[:], parts[:, 1, :], ALU.subtract).then_inc(split, 1)
                hold(dve, split, j + 1, k.vector_held)
            if bias_row is not None:
                dve.wait_ge(bias_in, 16)
            for t in range(AT_ONCE):
                finish(t, t, psG[:, t, :])
            with dve.Fori(1, NT // RING) as g:
                for u in range(RING):
                    finish(g * RING + u, u, ps[u][:])


def logit_factors(nc, k, s, kT, Xf, Xa, W1, W2, W3, q_rows):
    room = Room(nc, k.after_kT)
    w1 = room.take(f"lf{s}_w1", [P, FT, DA], F32)
    w2 = room.take(f"lf{s}_w2", [DA, DA], F32)
    w3 = room.take(f"lf{s}_w3", [P, FT, DA], F32)
    xf = [room.take(f"lf{s}_xf{u}", [P, D], F32) for u in range(SLOTS)]
    xa = [room.take(f"lf{s}_xa{u}", [P, D], F32) for u in range(SLOTS)]
    xT = [room.take(f"lf{s}_xT{u}", [P, FT, P], F32) for u in range(SLOTS)]
    q0 = [room.take(f"lf{s}_q0{u}", [DA, P], F32) for u in range(SLOTS)]
    q2 = room.take(f"lf{s}_q2", [DA, N], F32)
    rest = room.take(f"lf{s}_rest", [P, D], F32)
    w_in = nc.alloc_semaphore(f"lf{s}_w_in")
    X_in = nc.alloc_semaphore(f"lf{s}_X_in")
    xf_in = [nc.alloc_semaphore(f"lf{s}_xf_in{u}") for u in range(SLOTS)]
    xa_in = [nc.alloc_semaphore(f"lf{s}_xa_in{u}") for u in range(SLOTS)]
    split = nc.alloc_semaphore(f"lf{s}_split")
    turned = nc.alloc_semaphore(f"lf{s}_turned")
    xT_ready = nc.alloc_semaphore(f"lf{s}_xT_ready")
    kq_summed = nc.alloc_semaphore(f"lf{s}_kq_summed")
    q0_ready = nc.alloc_semaphore(f"lf{s}_q0_ready")
    q2_summed = nc.alloc_semaphore(f"lf{s}_q2_summed")
    q2_ready = nc.alloc_semaphore(f"lf{s}_q2_ready")
    q2_out = nc.alloc_semaphore(f"lf{s}_q2_out")
    vec = nc.alloc_semaphore(f"lf{s}_vec")
    with ExitStack() as ctx:
        psT = [ctx.enter_context(nc.psum_tensor(f"lf{s}_psT{u}", [P, FT, P], F32)) for u in range(SLOTS)]
        psK = [ctx.enter_context(nc.psum_tensor(f"lf{s}_psK{u}", [P, 512], F32)) for u in range(SLOTS)]
        psQ = [ctx.enter_context(nc.psum_tensor(f"lf{s}_psQ{u}", [P, 512], F32)) for u in range(SLOTS)]
        psR = [ctx.enter_context(nc.psum_tensor(f"lf{s}_psR{u}", [P, 512], F32)) for u in range(SLOTS)]
        block = ctx.enter_context(nc.Block())

        @block.sync
        def _(sp):
            sp.dma_start(w1[:], in_blocks(W1)).then_inc(w_in, 16)
            sp.dma_start(w3[:], in_blocks(W3)).then_inc(w_in, 16)
            sp.dma_start(w2[:], W2).then_inc(w_in, 16)
            with sp.Fori(0, NT // SLOTS) as g:
                for u in range(SLOTS):
                    t = g * SLOTS + u
                    sp.wait_ge(turned, freed(t))
                    sp.dma_start(xa[u][:], tile_rows(Xa, t)).then_inc(xa_in[u], 16)
                    if Xf is not None:
                        sp.wait_ge(split, freed(t))
                        sp.dma_start(xf[u][:], tile_rows(Xf, t)).then_inc(xf_in[u], 16)
            if Xf is None:
                sp.dma_start(k.X[:], Xa.rearrange("(t p) d -> p t d", p=P)).then_inc(X_in, 16)
            sp.wait_ge(q2_ready, done(NT - 1))
            sp.dma_start(q_rows, q2[:]).then_inc(q2_out, 16)
            sp.wait_ge(q2_out, 16)
            if Xf is None:
                sp.wait_ge(X_in, 16)

        @block.tensor
        def _(pe):
            pe.sem_inc(turned, SLOTS)
            pe.sem_inc(kq_summed, SLOTS)
            pe.sem_inc(q2_summed, SLOTS)
            pe.wait_ge(w_in, 48)
            with pe.Fori(0, NT // SLOTS) as g:
                for u in range(SLOTS):
                    t = g * SLOTS + u
                    pe.wait_ge(xa_in[u], g * 16 + 16)
                    pe.wait_ge(xT_ready, freed(t))
                    transpose_tile(nc, psT[u], xa[u], k.ident).then_inc(turned, 1)
                for u in range(SLOTS):
                    t = g * SLOTS + u
                    pe.wait_ge(xT_ready, done(t))
                    pe.wait_ge(q0_ready, freed(t))
                    for w, ps in ((w3, psK[u]), (w1, psQ[u])):
                        for f in range(FT):
                            last = nc.tensor.matmul(ps[0:DA, 0:P], w[:, f, :], xT[u][:, f, :],
                                                    start=f == 0, stop=f == FT - 1)
                    last.then_inc(kq_summed, 1)
                for u in range(SLOTS):
                    t = g * SLOTS + u
                    pe.wait_ge(q0_ready, done(t))
                    hold(pe, q2_ready, freed(t), k.tensor_held)
                    nc.tensor.matmul(psR[u][0:DA, 0:P], w2[:], q0[u][:], start=True, stop=True).then_inc(q2_summed, 1)

        @block.scalar
        def _(act):
            act.sem_inc(xT_ready, SLOTS)
            act.sem_inc(q0_ready, SLOTS)
            act.sem_inc(q2_ready, SLOTS)
            with act.Fori(0, NT // SLOTS) as g:
                for u in range(SLOTS):
                    t = g * SLOTS + u
                    act.wait_ge(turned, done(t))
                    act.wait_ge(kq_summed, freed(t))
                    nc.scalar.copy(xT[u][:], psT[u][:]).then_inc(xT_ready, 1)
                for u in range(SLOTS):
                    t = g * SLOTS + u
                    act.wait_ge(kq_summed, done(t))
                    nc.scalar.copy(kT[:, DS(t * P, P)], psK[u][0:DA, 0:P])
                    act.wait_ge(q2_summed, freed(t))
                    nc.scalar.copy(q0[u][:], psQ[u][0:DA, 0:P]).then_inc(q0_ready, 1)
                for u in range(SLOTS):
                    t = g * SLOTS + u
                    act.wait_ge(q2_summed, done(t))
                    nc.scalar.copy(q2[:, DS(t * P, P)], psR[u][0:DA, 0:P]).then_inc(q2_ready, 1)


        if Xf is not None:

            @block.vector
            def _(dve):
                dve.sem_inc(split, SLOTS)
                with dve.Fori(0, NT // SLOTS) as g:
                    for u in range(SLOTS):
                        t = g * SLOTS + u
                        ch = Chain(dve, vec)
                        dve.wait_ge(xf_in[u], g * 16 + 16)
                        parts = k.X3[:, t, :, :]
                        ch.link(copied_by_vector(nc, parts[:, 0, :], xf[u][:]))
                        ch.link(nc.vector.tensor_tensor(rest[:], xf[u][:], parts[:, 0, :], ALU.subtract))
                        ch.link(copied_by_vector(nc, parts[:, 1, :], rest[:]))
                        nc.vector.tensor_tensor(parts[:, 2, :], rest[:], parts[:, 1, :], ALU.subtract).then_inc(split, 1)
                        hold(dve, split, done(t), k.vector_held)


def move_mid(eng, ch, i, over, tmp, low, mid, step):
    if i + 1 < len(OCTAVE_STEPS):
        factor = 2.0 ** OCTAVE_STEPS[i + 1]
        ch.link(eng.tensor_scalar(tmp, over, factor - 1.0 / factor, 1.0 / factor, ALU.mult, ALU.add))
        ch.link(eng.tensor_tensor(mid, mid, tmp, ALU.mult))
    else:
        ch.link(eng.tensor_scalar(tmp, over, 0.5, 0.5, ALU.mult, ALU.add))
        ch.link(eng.tensor_tensor(low, mid, tmp, ALU.mult))
        ch.link(eng.tensor_scalar(step, low, 0.5, None, ALU.mult))
        ch.link(eng.tensor_tensor(mid, low, step, ALU.add))


def nucleus_step(nc, k, s, kT, q_rows, Xa_next, Xf):
    room = Room(nc, k.after_kT)
    PAIR = 2
    E = [[room.take(f"nu{s}_E{v}{a}", [P, N], F32) for a in range(PAIR)] for v in range(SLOTS)]
    unused_ahead = nc.alloc_sbuf_tensor_at(f"nu{s}_unused_ahead", [P, N], BF16, offset=room.at)
    WT = [room.take(f"nu{s}_WT{u}", [P, 4, P], F32) for u in range(SLOTS)]
    inside = nc.alloc_sbuf_tensor_at(f"nu{s}_inside", [P, N], F32, offset=room.at)
    tie = room.take(f"nu{s}_tie", [P, N], BF16)
    rank = room.take(f"nu{s}_rank", [P, N], F16)
    assert N * 4 == 2 * N * 2
    qT = [room.take(f"nu{s}_qT{u}", [DA, P], F32) for u in range(SLOTS)]
    xf_out = room.take(f"nu{s}_xf_out", [P, D], F32)
    hop = [room.take(f"nu{s}_hop{u}", [P, D], F32) for u in range(SLOTS)]
    xa_out = room.take(f"nu{s}_xa_out", [P, D], F32)
    top = room.take(f"nu{s}_top", [P, NT], F32)
    minus_top = room.take(f"nu{s}_minus_top", [P, NT], F32)
    mass = room.take(f"nu{s}_mass", [P, NT], F32)
    rnorm = room.take(f"nu{s}_rnorm", [P, NT], F32)
    largest8 = room.take(f"nu{s}_largest8", [P, PAIR, TOP], F32)
    sums8 = room.take(f"nu{s}_sums8", [P, PAIR, TOP], F32)
    doubts = room.take(f"nu{s}_doubts", [P, 2, PAIR], F32)
    doubts_all = room.take(f"nu{s}_doubts_all", [P, 2, PAIR], F32)
    found = room.take(f"nu{s}_found", [P, 2], F32)
    AHEAD = PROBES_AHEAD[s]
    state = room.take(f"nu{s}_state", [P, SLOTS, 4, PAIR], F32)
    small = room.take(f"nu{s}_small", [P, 6, PAIR], F32)
    above, over, tmp, count, most, rest = [small[:, n, :] for n in range(6)]
    p_top = room.take(f"nu{s}_p_top", [P, PAIR], F32)
    ahead_small = room.take(f"nu{s}_ahead_small", [P, 6, PAIR], F32)
    minus_mid, relus, signs, ahead_over, ahead_mass, ahead_tmp = [ahead_small[:, n, :] for n in range(6)]
    qT_in = [nc.alloc_semaphore(f"nu{s}_qT_in{u}") for u in range(SLOTS)]
    logits_summed = nc.alloc_semaphore(f"nu{s}_logits_summed")
    top_ready = nc.alloc_semaphore(f"nu{s}_top_ready")
    exp_done = nc.alloc_semaphore(f"nu{s}_exp_done")
    xf_summed = nc.alloc_semaphore(f"nu{s}_xf_summed")
    xf_copied = nc.alloc_semaphore(f"nu{s}_xf_copied")
    xf_stored = nc.alloc_semaphore(f"nu{s}_xf_stored")
    weights_ready = nc.alloc_semaphore(f"nu{s}_weights_ready")
    turned = nc.alloc_semaphore(f"nu{s}_turned")
    WT_ready = nc.alloc_semaphore(f"nu{s}_WT_ready")
    WT_used = nc.alloc_semaphore(f"nu{s}_WT_used")
    xa_copied = nc.alloc_semaphore(f"nu{s}_xa_copied")
    xa_stored = nc.alloc_semaphore(f"nu{s}_xa_stored")
    hop_in = [nc.alloc_semaphore(f"nu{s}_hop_in{u}") for u in range(SLOTS)]
    hop_split = nc.alloc_semaphore(f"nu{s}_hop_split")
    hop_steps = nc.alloc_semaphore(f"nu{s}_hop_steps")
    vec = nc.alloc_semaphore(f"nu{s}_vec")
    top_found = nc.alloc_semaphore(f"nu{s}_top_found")
    mid_ready = nc.alloc_semaphore(f"nu{s}_mid_ready")
    probed_ahead = nc.alloc_semaphore(f"nu{s}_probed_ahead")
    searched = nc.alloc_semaphore(f"nu{s}_searched")
    act_steps = nc.alloc_semaphore(f"nu{s}_act_steps")
    pool_steps = nc.alloc_semaphore(f"nu{s}_pool_steps")
    p_top_set = nc.alloc_semaphore(f"nu{s}_p_top_set")
    proof_ready = nc.alloc_semaphore(f"nu{s}_proof_ready")
    proof_reduced = nc.alloc_semaphore(f"nu{s}_proof_reduced")
    NP = NT // PAIR
    GROUPS = NT // 4
    HOP_START = (range(0, 2), range(3, 5))[s]
    HOP_END = ((2,), ())[s]
    BOTH_HOPS = s == STEPS - 1
    BEFORE = HOP_START[0] * PAIR

    def hops_after(p):
        if not BOTH_HOPS or isinstance(p, int) and p == 1:
            return ()
        return range(5, NP) if isinstance(p, int) and p == 0 else (p * 2 + 4, p * 2 + 5)

    with ExitStack() as ctx:
        banks = ctx.enter_context(nc.psum_tensor(f"nu{s}_banks", [P, 8, D], F32))
        psL = banks[:, 0:NQ, :].rearrange("p b n -> p (b n)")
        psL_second = banks[:, NQ:2 * NQ, :].rearrange("p b n -> p (b n)")
        psF = banks[:, 4, :]
        psA = banks[:, 5, :]
        psT = [banks[:, 6 + u, :].rearrange("p (n q) -> p n q", n=4) for u in range(SLOTS)]
        block = ctx.enter_context(nc.Block())

        @block.sync
        def _(sp):
            def load_q(p):
                for a in range(PAIR):
                    t = p * PAIR + a
                    sp.wait_ge(logits_summed, freed(t))
                    sp.dma_start(qT[a][:], q_rows[:, DS(t * P, P)]).then_inc(qT_in[a], 16)

            def store_xa(p):
                for a in range(PAIR):
                    t = p * PAIR + a
                    sp.wait_ge(xa_copied, t + 2)
                    sp.dma_start(tile_rows(Xa_next, t), xa_out[:]).then_inc(xa_stored, 16)

            def store_xf(p, which=1):
                for a in range(PAIR):
                    t = p * PAIR + a
                    sp.wait_ge(xf_copied, t + 2)
                    sp.dma_start(tile_rows(Xf[which], t - (which - 1) * NT), xf_out[:]).then_inc(xf_stored, 16)

            sp.sem_inc(xf_stored, 16 * (BEFORE + 1))
            sp.sem_inc(xa_stored, 16)
            for p in range(3):
                load_q(p)
            for m in HOP_START:
                store_xf(m)
            for p in range(2):
                store_xa(p)
                load_q(p + 3)
                for m in hops_after(p):
                    store_xf(m)
            with sp.Fori(2, NP - 3) as p:
                store_xa(p)
                load_q(p + 3)
                for m in hops_after(p):
                    store_xf(m, 2)
            store_xa(NP - 3)
            for m in hops_after(NP - 3):
                store_xf(m, 2)
            store_xa(NP - 2)
            for m in HOP_END:
                store_xf(m)
            store_xa(NP - 1)
            sp.wait_ge(xf_stored, 16 * ((STEPS * NT if BOTH_HOPS else (len(HOP_START) + len(HOP_END)) * PAIR) + 1))
            sp.wait_ge(xa_stored, 16 * (NT + 1))

        @block.tensor
        def _(pe):
            def logits(p, a, out=psL, read=None):
                t = p * PAIR + a
                pe.wait_ge(qT_in[a], p * 16 + 16)
                pe.wait_ge(exp_done, t + 1 if read is None else read)
                for c in range(NQ):
                    last = nc.tensor.matmul(out[:, c * 512:(c + 1) * 512], qT[a][:], kT[:, c * 512:(c + 1) * 512],
                                            start=True, stop=True)
                last.then_inc(logits_summed, 1)

            def neighbours(p, which=1):
                for a in range(PAIR):
                    t = p * PAIR + a
                    node = t - (which - 1) * NT
                    pe.wait_ge(xf_copied, t + 1)
                    for n in range(PARTS):
                        nc.tensor.matmul(psF, k.identb[:], k.X3[:, node, n, :], start=n == 0, stop=False)
                    for j in range(NT):
                        for n in range(PARTS):
                            last = nc.tensor.matmul(psF, k.AT[:, j, DS(node * P, P)], k.X3[:, j, n, :],
                                                    start=False, stop=j == NT - 1 and n == PARTS - 1)
                    last.then_inc(xf_summed, 1)

            def apply(p, v, a):
                t = p * PAIR + a
                pe.wait_ge(weights_ready, t + 1)
                pe.wait_ge(xa_copied, t + 1)
                for c in range(GROUPS + 1):
                    if c < GROUPS:
                        pe.wait_ge(WT_ready, freed(t * GROUPS + c))
                        for n in range(4):
                            last = nc.tensor.transpose(psT[c % 2][:, n, :],
                                                       E[v][a][:, (c * 4 + n) * P:(c * 4 + n + 1) * P], k.ident[:])
                        last.then_inc(turned, 1)
                    if c:
                        pe.wait_ge(WT_ready, done(t * GROUPS + c - 1))
                        for n in range(4):
                            j = (c - 1) * 4 + n
                            last = nc.tensor.matmul(psA, WT[(c - 1) % 2][:, n, :], k.X[:, j, :], start=j == 0,
                                                    stop=j == NT - 1)
                        last.then_inc(WT_used, 1)

            pe.sem_inc(WT_used, SLOTS)
            if BEFORE:
                pe.sem_inc(xf_summed, BEFORE)
            pe.sem_inc(logits_summed, SLOTS)
            logits(0, 0)
            logits(0, 1, psL_second, 1)
            logits(1, 0, psL, 2)
            logits(1, 1)
            for m in HOP_START:
                neighbours(m)

            def pair(p, v):
                logits(p + 2, 0)
                apply(p, v, 0)
                logits(p + 2, 1)
                apply(p, v, 1)

            for p in range(2):
                pair(p, p)
                for m in hops_after(p):
                    neighbours(m)
            with pe.Fori(1, NP // SLOTS - 1) as g:
                for v in range(SLOTS):
                    pair(g * SLOTS + v, v)
                    if BOTH_HOPS:
                        pe.wait_ge(hop_split, NT)
                    for m in hops_after(g * SLOTS + v):
                        neighbours(m, 2)
            for a in range(PAIR):
                apply(NP - 2, 0, a)
            for m in HOP_END:
                neighbours(m)
            for a in range(PAIR):
                apply(NP - 1, 1, a)

        @block.scalar
        def _(act):
            def exponentials(p, v, a, src=psL):
                t = p * PAIR + a
                act.wait_ge(logits_summed, done(t))
                act.wait_ge(top_ready, t + 1)
                nc.scalar.activation(E[v][a][:], src, ACT.Exp, bias=minus_top[:, DS(t, 1)],
                                     accum_out=mass[:, DS(t, 1)]).then_inc(exp_done, 1)

            def probe_ahead(p, v, i):
                for a in range(PAIR):
                    ch = Chain(act, act_steps)
                    hold(act, mid_ready, (p * AHEAD + i) * PAIR + a + 1, k.scalar_held)
                    for function, sums in ((ACT.Relu, relus), (ACT.Sign, signs)):
                        ch.link(nc.scalar.activation(unused_ahead[:], E[v][a][:], function, bias=minus_mid[:, a:a + 1],
                                                     accum_out=sums[:, a:a + 1]))
                    act.sem_inc(probed_ahead, 1)

            def copy_xf(t, which=1):
                node = t - (which - 1) * NT
                act.wait_ge(xf_summed, t + 1)
                act.wait_ge(xf_stored, 16 * t + 16)
                nc.scalar.activation(xf_out[:], psF, ACT.Copy, scale=k.rscale[:, DS(node, 1)]).then_inc(xf_copied, 1)

            def search_and_copy(p, v, hops, which=1):
                tiles = [m * PAIR + a for m in hops for a in range(PAIR)]
                for i in range(max(AHEAD, len(tiles))):
                    if i < AHEAD:
                        probe_ahead(p, v, i)
                    if i < len(tiles):
                        copy_xf(tiles[i], which)

            def copy_weights(p, a):
                t = p * PAIR + a
                for c in range(GROUPS):
                    act.wait_ge(turned, t * GROUPS + c + 1)
                    act.wait_ge(WT_used, freed(t * GROUPS + c))
                    nc.scalar.copy(WT[c % 2][:], psT[c % 2]).then_inc(WT_ready, 1)

            def copy_xa(p, a):
                t = p * PAIR + a
                act.wait_ge(WT_used, done(t * GROUPS + GROUPS - 1))
                act.wait_ge(xa_stored, 16 * t + 16)
                nc.scalar.activation(xa_out[:], psA, ACT.Copy, scale=rnorm[:, DS(t, 1)]).then_inc(xa_copied, 1)

            act.sem_inc(exp_done, 1)
            act.sem_inc(xf_copied, BEFORE + 1)
            act.sem_inc(xa_copied, 1)
            act.sem_inc(WT_ready, SLOTS)
            for v in range(SLOTS):
                for a in range(PAIR):
                    exponentials(v, v, a, psL_second if (v, a) == (0, 1) else psL)
                search_and_copy(v, v, ())
            for m in HOP_START:
                for a in range(PAIR):
                    copy_xf(m * PAIR + a)

            def pair(p, v):
                for a in range(PAIR):
                    copy_weights(p, a)
                    exponentials(p + 2, v, a)
                    copy_xa(p, a)

            for p in range(2):
                pair(p, p)
                search_and_copy(p + 2, p, hops_after(p))
            with act.Fori(1, NP // SLOTS - 1) as g:
                for v in range(SLOTS):
                    pair(g * SLOTS + v, v)
                    search_and_copy(g * SLOTS + v + 2, v, hops_after(g * SLOTS + v), 2)
            for a in range(PAIR):
                copy_weights(NP - 2, a)
                copy_xa(NP - 2, a)
            for m in HOP_END:
                for a in range(PAIR):
                    copy_xf(m * PAIR + a)
            for a in range(PAIR):
                copy_weights(NP - 1, a)
                copy_xa(NP - 1, a)

        @block.gpsimd
        def _(pool):
            def search(p, v, doubts_of=None):
                goal, low, mid, step = [state[:, v, n, :] for n in range(4)]
                hold(pool, exp_done, p * PAIR + PAIR + 1, k.pool_held)
                ch = Chain(pool, pool_steps)
                ch.link(nc.gpsimd.tensor_tensor(goal, mass[:, DS(p * PAIR, PAIR)], p_top[:], ALU.mult))
                ch.link(nc.gpsimd.memset(mid, LOWEST * 2.0 ** OCTAVE_STEPS[0]))
                ch.link(nc.gpsimd.memset(minus_mid, -LOWEST * 2.0 ** OCTAVE_STEPS[0]))
                pool.sem_inc(mid_ready, PAIR)
                for i in range(AHEAD):
                    if i == AHEAD - 1 and doubts_of is not None:
                        reduce_doubts(doubts_of)
                        ch = Chain(pool, pool_steps)
                    for a in range(PAIR):
                        hold(pool, probed_ahead, (p * AHEAD + i) * PAIR + a + 1, k.pool_held)
                        col = slice(a, a + 1)
                        half, over_a = ahead_mass[:, col], ahead_over[:, col]
                        ch.link(nc.gpsimd.tensor_scalar(half, signs[:, col], float(N), 0.5, ALU.add, ALU.mult))
                        ch.link(nc.gpsimd.tensor_tensor(half, half, mid[:, col], ALU.mult))
                        ch.link(nc.gpsimd.tensor_tensor(half, half, relus[:, col], ALU.add))
                        ch.link(nc.gpsimd.tensor_scalar(over_a, half, goal[:, col], None, ALU.is_ge))
                        move_mid(nc.gpsimd, ch, i, over_a, ahead_tmp[:, col], low[:, col], mid[:, col], step[:, col])
                        ch.link(nc.gpsimd.tensor_scalar(minus_mid[:, col], mid[:, col], -1.0, None, ALU.mult))
                        pool.sem_inc(mid_ready if i + 1 < AHEAD else searched, 1)

            def reduce_doubts(p):
                hold(pool, proof_ready, p + 1, k.pool_held)
                nc.gpsimd.partition_all_reduce(doubts_all[:].rearrange("p n a -> p (n a)"),
                                               doubts[:].rearrange("p n a -> p (n a)"), P, RMAX).then_inc(proof_reduced, 1)

            def split_hop(first, end):
                pool.wait_ge(xf_summed, NT)
                pool.wait_ge(xf_stored, 16 * (NT + 1))

                def load(t, u):
                    nc.gpsimd.dma_start(hop[u][:], tile_rows(Xf[1], t)).then_inc(hop_in[u], 16)

                def split(t, u, ahead=True):
                    ch = Chain(pool, hop_steps)
                    if ahead:
                        load(t + 1, 1 - u)
                    hold(pool, hop_in[u], (t - u) * 8 + 16, k.pool_held)
                    parts = k.X3[:, t, :, :]
                    for n in range(PARTS - 1):
                        ch.link(nc.gpsimd.tensor_copy(parts[:, n, :], hop[u][:]))
                        ch.link(nc.gpsimd.tensor_tensor(parts[:, PARTS - 1, :] if n == PARTS - 2 else hop[u][:],
                                                        hop[u][:], parts[:, n, :], ALU.subtract))
                    pool.sem_inc(hop_split, 1)

                load(first, 0)
                with pool.Fori(first // SLOTS, end // SLOTS - 1) as g:
                    for u in range(SLOTS):
                        split(g * SLOTS + u, u)
                split(end - 2, 0)
                split(end - 1, 1, False)

            nc.gpsimd.memset(p_top[:], P_TOP).then_inc(p_top_set, 1)
            pool.wait_ge(p_top_set, 1)
            search(0, 0)
            search(1, 1)
            reduce_doubts(0)
            for p in range(2):
                search(p + 2, p, p + 1)
                if BOTH_HOPS:
                    split_hop(p * NT // 2, (p + 1) * NT // 2)
            with pool.Fori(2, NP // SLOTS) as g:
                for v in range(SLOTS):
                    search(g * SLOTS + v, v, g * SLOTS + v - 1)
            reduce_doubts(NP - 1)

        @block.vector
        def _(dve):
            def largest(p, a, src=psL):
                t = p * PAIR + a
                dve.wait_ge(logits_summed, done(t))
                nc.vector.tensor_reduce(top[:, DS(t, 1)], src, AX.X, ALU.max).then_inc(top_found, 1)
                dve.wait_ge(top_found, t + 1)
                nc.vector.tensor_scalar(minus_top[:, DS(t, 1)], top[:, DS(t, 1)], -1.0, None,
                                        ALU.mult).then_inc(top_ready, 1)

            def probe(ch, v, mid, goal):
                for a, unused in enumerate((tie, rank)):
                    ch.add(nc.vector.scalar_tensor_tensor(unused[:], E[v][a][:], mid[:, a:a + 1], E[v][a][:],
                                                          ALU.is_ge, ALU.mult, accum_out=above[:, a:a + 1]))
                dve.wait_ge(vec, ch.n)
                ch.link(nc.vector.tensor_tensor(over, above, goal, ALU.is_ge))

            def mantissa_bit(v):
                goal, low, mid, step = [state[:, v, n, :] for n in range(4)]
                """mid moves by half a step to the side of it on which T is; T's bracket is mid +- step."""
                bit = Chain(dve, vec)
                probe(bit, v, mid, goal)
                bit.link(nc.vector.scalar_tensor_tensor(tmp, over, -0.5, step, ALU.add, ALU.mult))
                bit.add(nc.vector.tensor_scalar(step, step, 0.5, None, ALU.mult))
                bit.link(nc.vector.tensor_tensor(mid, mid, tmp, ALU.add))

            def look_inside(v):
                goal, low, mid, step = [state[:, v, n, :] for n in range(4)]
                ch = Chain(dve, vec)
                ch.link(nc.vector.tensor_tensor(low, mid, step, ALU.subtract))
                ch.link(nc.vector.tensor_tensor(mid, mid, step, ALU.add))
                for a in range(PAIR):
                    ch.link(nc.vector.scalar_tensor_tensor(inside[:], E[v][a][:], mid[:, a:a + 1], E[v][a][:],
                                                           ALU.is_le, ALU.mult, accum_out=above[:, a:a + 1]))
                    ch.link(nc.vector.max(largest8[:, a, :], inside[:]))
                ch.link(nc.vector.tensor_tensor(tmp, above, rest, ALU.subtract))
                for a in range(PAIR):
                    ch.link(nc.vector.tensor_tensor_scan(sums8[:, a, :], largest8[:, a, :], largest8[:, a, :], 0.0,
                                                         ALU.add, ALU.max))
                    ch.link(nc.vector.scalar_tensor_tensor(sums8[:, a, :], sums8[:, a, :], tmp[:, a:a + 1],
                                                           largest8[:, a, :], ALU.is_ge, ALU.mult))
                ch.link(nc.vector.tensor_reduce(mid, sums8[:], AX.X, ALU.max))
                ch.link(nc.vector.tensor_tensor(mid, mid, largest8[:, :, TOP - 1], ALU.max))
                ch.link(nc.vector.tensor_tensor(mid, mid, low, ALU.max))
                probe(ch, v, mid, goal)

            def select(p, v, ahead=None):
                goal, low, mid, step = [state[:, v, n, :] for n in range(4)]
                ch = Chain(dve, vec)
                dve.wait_ge(searched, p * PAIR + PAIR)
                ch.link(nc.vector.tensor_tensor(rest, mass[:, DS(p * PAIR, PAIR)], goal, ALU.subtract))
                for i in range(AHEAD, len(OCTAVE_STEPS)):
                    probe(ch, v, mid, goal)
                    move_mid(nc.vector, ch, i, over, tmp, low, mid, step)
                for _ in range(FIRST_BITS[s] % UNROLLED_BITS or UNROLLED_BITS):
                    mantissa_bit(v)
                if ahead is not None:
                    largest(ahead, 1)
                if FIRST_BITS[s] > UNROLLED_BITS:
                    with dve.Fori(0, (FIRST_BITS[s] - 1) // UNROLLED_BITS):
                        for _ in range(UNROLLED_BITS):
                            mantissa_bit(v)
                look_inside(v)
                ch = Chain(dve, vec)
                ch.add(nc.vector.tensor_scalar(doubts[:, 0, :], over, -1.0, 1.0, ALU.mult, ALU.add))
                ch.link(nc.vector.tensor_tensor(tmp, above, mid, ALU.subtract))
                nc.vector.tensor_tensor(doubts[:, 1, :], tmp, goal, ALU.is_ge).then_inc(proof_ready, 1)
                hold(dve, proof_reduced, p + 1, k.vector_held)
                ch.add(nc.vector.tensor_reduce(found[:, 0:1], doubts_all[:, 0, :], AX.X, ALU.max))
                ch.link(nc.vector.tensor_reduce(found[:, 1:2], doubts_all[:].rearrange("p n a -> p (n a)"), AX.X, ALU.max))
                any_open, any_doubt = [dve.value_load(found[0:1, n:n + 1].bitcast(mybir.dt.int32)) for n in range(2)]
                with dve.If(any_open):
                    ch = Chain(dve, vec)
                    ch.link(nc.vector.scalar_tensor_tensor(mid, step, 2.0, low, ALU.mult, ALU.add))
                    probe(ch, v, mid, goal)
                    ch.link(nc.vector.tensor_tensor(tmp, over, mid, ALU.mult))
                    ch.link(nc.vector.tensor_tensor(low, low, tmp, ALU.max))
                    ch.link(nc.vector.tensor_tensor(mid, low, step, ALU.add))
                    with dve.Fori(0, MANTISSA_STEPS - 1 - FIRST_BITS[s]):
                        mantissa_bit(v)
                    ch = Chain(dve, vec)
                    probe(ch, v, mid, goal)
                    ch.link(nc.vector.scalar_tensor_tensor(tmp, over, -1.0, step, ALU.add, ALU.mult))
                    ch.link(nc.vector.tensor_tensor(mid, mid, tmp, ALU.add))
                    probe(ch, v, mid, goal)
                with dve.If(any_doubt):
                    ch = Chain(dve, vec)
                    ch.link(nc.vector.reciprocal(tmp, mid))
                    ch.link(nc.vector.tensor_tensor(over, goal, above, ALU.subtract))
                    ch.link(nc.vector.tensor_tensor(over, over, tmp, ALU.mult))
                    for a in range(PAIR):
                        T = mid[:, a:a + 1]
                        ch.link(nc.vector.tensor_scalar(tie[:], E[v][a][:], T, None, ALU.is_equal))
                        ch.link(nc.vector.tensor_tensor_scan(rank[:], tie[:], tie[:], 0.0, ALU.add, ALU.max))
                        ch.add(nc.vector.scalar_tensor_tensor(most[:, a:a + 1], rank[:, N - 1:N], 1.0,
                                                              over[:, a:a + 1], ALU.add, ALU.add))
                        ch.link(nc.vector.scalar_tensor_tensor(E[v][a][:], E[v][a][:], T, E[v][a][:],
                                                               ALU.is_gt, ALU.mult))
                        ch.link(nc.vector.scalar_tensor_tensor(tie[:], rank[:], most[:, a:a + 1], tie[:],
                                                               ALU.is_lt, ALU.mult))
                        ch.link(nc.vector.scalar_tensor_tensor(E[v][a][:], tie[:], T, E[v][a][:], ALU.mult, ALU.add,
                                                               accum_out=count[:, a:a + 1]))
                with dve.Else():
                    ch = Chain(dve, vec)
                    for a in range(PAIR):
                        ch.link(nc.vector.scalar_tensor_tensor(E[v][a][:], E[v][a][:], mid[:, a:a + 1], E[v][a][:],
                                                               ALU.is_ge, ALU.mult, accum_out=count[:, a:a + 1]))
                for a in range(PAIR):
                    nc.vector.reciprocal(rnorm[:, DS(p * PAIR + a, 1)], count[:, a:a + 1]).then_inc(weights_ready, 1)

            for t in range(2 * PAIR - 1):
                largest(t // PAIR, t % PAIR, psL_second if t == 1 else psL)
            if AHEAD > 1:
                select(0, 0, 1)
            else:
                largest(1, 1)
                select(0, 0)
            with dve.Fori(0, NP // SLOTS - 1) as g:
                for v in range(SLOTS):
                    p = g * SLOTS + v
                    largest(p + 2, 0)
                    select(p + 1, 1 - v, p + 2)
            select(NP - 1, 1)


def combine_steps(nc, k, x2, Xf, Xa, U1, U2, gamma, beta, x3):
    room = Room(nc, k.start)
    terms = [w for s in range(STEPS) for w in ((Xf[s + 1], U1[s]), (Xa[s + 1], U2[s]))]
    M = len(terms)
    w = [room.take(f"cs_w{n}", [P, FT, D], F32) for n in range(M)]
    gr = room.take("cs_gamma", [P, D], F32)
    br = room.take("cs_beta", [P, D], F32)
    x = [room.take(f"cs_x{u}", [P, D], F32) for u in range(SLOTS)]
    y = room.take("cs_y", [P, D], F32)
    xin = [room.take(f"cs_in{u}", [P, D], F32) for u in range(M)]
    xT = [room.take(f"cs_xT{u}", [P, FT, P], F32) for u in range(SLOTS)]
    stats = room.take("cs_stats", [P, 6], F32)
    mv = room.take("cs_mv", [P, 2], F32)
    sd = room.take("cs_sd", [P, 1], F32)
    rstd = room.take("cs_rstd", [P, 1], F32)
    w_in = [nc.alloc_semaphore(f"cs_w_in{n}") for n in range(M)]
    rows_in = nc.alloc_semaphore("cs_rows_in")
    x_in = [nc.alloc_semaphore(f"cs_x_in{u}") for u in range(SLOTS)]
    x3_out = [nc.alloc_semaphore(f"cs_x3_out{u}") for u in range(SLOTS)]
    in_in = [nc.alloc_semaphore(f"cs_in_in{u}") for u in range(M)]
    turned = nc.alloc_semaphore("cs_turned")
    xT_ready = nc.alloc_semaphore("cs_xT_ready")
    projected = nc.alloc_semaphore("cs_projected")
    taken = nc.alloc_semaphore("cs_taken")
    var_ready = nc.alloc_semaphore("cs_var_ready")
    root_ready = nc.alloc_semaphore("cs_root_ready")
    x3_ready = nc.alloc_semaphore("cs_x3_ready")
    taken_x = nc.alloc_semaphore("cs_taken_x")
    vec = nc.alloc_semaphore("cs_vec")
    with ExitStack() as ctx:
        psT = [ctx.enter_context(nc.psum_tensor(f"cs_psT{u}", [P, FT, P], F32)) for u in range(SLOTS)]
        psY = [ctx.enter_context(nc.psum_tensor(f"cs_psY{u}", [P, D], F32)) for u in range(SLOTS)]
        block = ctx.enter_context(nc.Block())

        @block.sync
        def _(sp):
            def load_terms(t):
                for n, (rows, _) in enumerate(terms):
                    sp.wait_ge(turned, t * M + n + 1)
                    sp.dma_start(xin[n][:], tile_rows(rows, t)).then_inc(in_in[n], 16)

            load_terms(0)
            for n, (_, u) in enumerate(terms):
                sp.dma_start(w[n][:], in_blocks(u)).then_inc(w_in[n], 16)
            sp.dma_start(gr[:], gamma.partition_broadcast(P)).then_inc(rows_in, 16)
            sp.dma_start(br[:], beta.partition_broadcast(P)).then_inc(rows_in, 16)
            for u in range(SLOTS):
                sp.dma_start(x[u][:], tile_rows(x2, u)).then_inc(x_in[u], 16)
            load_terms(1)
            with sp.Fori(0, NT // SLOTS - 1) as g:
                for u in range(SLOTS):
                    load_terms((g + 1) * SLOTS + u)
                for u in range(SLOTS):
                    t = g * SLOTS + u
                    sp.wait_ge(x3_ready, t + 1)
                    sp.dma_start(tile_rows(x3, t), x[u][:]).then_inc(x3_out[u], 16)
                    sp.wait_ge(x3_out[u], g * 16 + 16)
                    sp.dma_start(x[u][:], tile_rows(x2, t + SLOTS)).then_inc(x_in[u], 16)
            for u in range(SLOTS):
                t = NT - SLOTS + u
                sp.wait_ge(x3_ready, t + 1)
                sp.dma_start(tile_rows(x3, t), x[u][:]).then_inc(x3_out[u], 16)
            for u in range(SLOTS):
                sp.wait_ge(x3_out[u], 16 * NT // SLOTS)

        @block.tensor
        def _(pe):
            pe.sem_inc(turned, M)
            pe.sem_inc(projected, SLOTS)
            def turn(t, n):
                pe.wait_ge(in_in[n], t * 16 + 16)
                pe.wait_ge(xT_ready, freed(t * M + n))
                transpose_tile(nc, psT[n % 2], xin[n], k.ident).then_inc(turned, 1)

            def tile(t, u, first=False, last=False):
                pe.wait_ge(taken, freed(t))
                for n in range(M):
                    if n + 1 < M:
                        turn(t, n + 1)
                    elif not last:
                        turn(t + 1, 0)
                    if first:
                        pe.wait_ge(w_in[n], 16)
                    pe.wait_ge(xT_ready, done(t * M + n))
                    project_tile(nc, psY[u][:], xT[n % 2], w[n], n == 0, n == M - 1).then_inc(projected, 1)

            turn(0, 0)
            tile(0, 0, first=True)
            tile(1, 1)
            with pe.Fori(1, NT // SLOTS - 1) as g:
                for u in range(SLOTS):
                    tile(g * SLOTS + u, u)
            tile(NT - 2, 0)
            tile(NT - 1, 1, last=True)

        @block.scalar
        def _(act):
            def copy_turned(t):
                for n in range(M):
                    act.wait_ge(turned, t * M + n + 1 + M)
                    act.wait_ge(projected, freed(t * M + n))
                    nc.scalar.copy(xT[n % 2][:], psT[n % 2][:]).then_inc(xT_ready, 1)

            def roots(t):
                for n in range(2):
                    act.wait_ge(var_ready, t * 2 + n + 1)
                    nc.scalar.activation(sd[:], mv[:, 1:2], ACT.Sqrt, bias=k.eps[:]).then_inc(root_ready, 1)

            act.sem_inc(xT_ready, SLOTS)
            copy_turned(0)
            with act.Fori(0, NT - 1) as t:
                copy_turned(t + 1)
                roots(t)
            roots(NT - 1)


        @block.vector
        def _(dve):
            dve.sem_inc(taken, SLOTS)
            dve.wait_ge(rows_in, 32)
            with dve.Fori(0, NT // SLOTS) as g:
                for u in range(SLOTS):
                    t = g * SLOTS + u
                    ch = Chain(dve, vec)
                    dve.wait_ge(x_in[u], g * 16 + 16)
                    dve.wait_ge(projected, done(t * M + M - 1))
                    nc.vector.tensor_tensor(y[:], x[u][:], psY[u][:], ALU.add).then_inc(taken, 1)
                    dve.wait_ge(taken, done(t))
                    for n in range(2):
                        ch.link(nc.vector.bn_stats(stats[:], y[:]))
                        nc.vector.bn_aggr(mv[:], stats[:]).then_inc(var_ready, 1)
                        dve.wait_ge(root_ready, t * 2 + n + 1)
                        ch.link(nc.vector.reciprocal(rstd[:], sd[:]))
                        if n == 0:
                            ch.link(nc.vector.tensor_scalar(y[:], y[:], mv[:, 0:1], rstd[:], ALU.subtract, ALU.mult))
                            ch.link(nc.vector.tensor_tensor(y[:], y[:], gr[:], ALU.mult))
                            ch.link(nc.vector.tensor_tensor(y[:], y[:], br[:], ALU.add))
                            nc.vector.tensor_tensor(y[:], y[:], x[u][:], ALU.add).then_inc(taken_x, 1)
                            dve.wait_ge(taken_x, t + 1)
                        else:
                            nc.vector.tensor_scalar(x[u][:], y[:], mv[:, 0:1], rstd[:], ALU.subtract,
                                                    ALU.mult).then_inc(x3_ready, 1)
                            hold(dve, x3_ready, t + 1, k.vector_held)


def support(nc, k, x3, weight):
    room = Room(nc, k.upper)
    w = room.take("su_w", [P, FT, D], F32)
    x = [room.take(f"su_x{u}", [P, D], F32) for u in range(SLOTS)]
    xT = [room.take(f"su_xT{u}", [P, FT, P], F32) for u in range(SLOTS)]
    w_in = nc.alloc_semaphore("su_w_in")
    x_in = [nc.alloc_semaphore(f"su_x_in{u}") for u in range(SLOTS)]
    turned = nc.alloc_semaphore("su_turned")
    xT_ready = nc.alloc_semaphore("su_xT_ready")
    projected = nc.alloc_semaphore("su_projected")
    taken = nc.alloc_semaphore("su_taken")
    with ExitStack() as ctx:
        psT = [ctx.enter_context(nc.psum_tensor(f"su_psT{u}", [P, FT, P], F32)) for u in range(SLOTS)]
        psY = [ctx.enter_context(nc.psum_tensor(f"su_psY{u}", [P, D], F32)) for u in range(SLOTS)]
        block = ctx.enter_context(nc.Block())

        @block.sync
        def _(sp):
            sp.dma_start(w[:], in_blocks(weight)).then_inc(w_in, 16)
            with sp.Fori(0, NT // SLOTS) as g:
                for u in range(SLOTS):
                    t = g * SLOTS + u
                    sp.wait_ge(turned, freed(t))
                    sp.dma_start(x[u][:], tile_rows(x3, t)).then_inc(x_in[u], 16)

        @block.tensor
        def _(pe):
            pe.sem_inc(turned, SLOTS)
            pe.sem_inc(projected, SLOTS)
            pe.wait_ge(w_in, 16)
            with pe.Fori(0, NT // SLOTS) as g:
                for u in range(SLOTS):
                    t = g * SLOTS + u
                    pe.wait_ge(x_in[u], g * 16 + 16)
                    pe.wait_ge(xT_ready, freed(t))
                    transpose_tile(nc, psT[u], x[u], k.ident).then_inc(turned, 1)
                for u in range(SLOTS):
                    t = g * SLOTS + u
                    pe.wait_ge(xT_ready, done(t))
                    pe.wait_ge(taken, freed(t))
                    project_tile(nc, psY[u][:], xT[u], w).then_inc(projected, 1)

        @block.scalar
        def _(act):
            act.sem_inc(xT_ready, SLOTS)
            with act.Fori(0, NT // SLOTS) as g:
                for u in range(SLOTS):
                    t = g * SLOTS + u
                    act.wait_ge(turned, done(t))
                    act.wait_ge(projected, freed(t))
                    nc.scalar.copy(xT[u][:], psT[u][:]).then_inc(xT_ready, 1)


        @block.vector
        def _(dve):
            dve.sem_inc(taken, SLOTS)
            with dve.Fori(0, NT // SLOTS) as g:
                for u in range(SLOTS):
                    t = g * SLOTS + u
                    dve.wait_ge(projected, done(t))
                    copied_by_vector(nc, k.X[:, t, :], psY[u][:]).then_inc(taken, 1)


def build(nc, x, adj, adjT, L0_gnn_W_seq, L0_gnn_a1, L0_gnn_a2, L0_gnn_W_out, L0_gnn_b_out, L2_gnn_W1, L2_gnn_W2,
          L2_gnn_W3, L2_gnn_U1_0, L2_gnn_U1_1, L2_gnn_U2_0, L2_gnn_U2_1, L2_gnn_gamma, L2_gnn_beta, L3_gnn_weight,
          L3_gnn_bias, out, upto=99):
    def scratch(name, shape):
        return nc.dram_tensor(name, shape, F32, kind="Internal").ap()

    s1_rows = scratch("s1_rows", [HEADS, N])
    x1 = scratch("x1", [N, D])
    x2 = scratch("x2", [N, D])
    x3 = scratch("x3", [N, D])
    q_rows = scratch("q_rows", [DA, N])
    Xf = [x2] + [scratch(f"Xf{s + 1}", [N, D]) for s in range(STEPS)]
    Xa = [x2] + [scratch(f"Xa{s + 1}", [N, D]) for s in range(STEPS)]
    k = Kept(nc)
    gat = Gat(nc, k)
    room = Room(nc, k.upper)
    kT = room.take("kT", [DA, N], F32)
    k.after_kT = room.at
    phases = [
        lambda: prepare_adjacency(nc, k, adjT),
        lambda: attention_scores(nc, k, gat, x, L0_gnn_W_seq, L0_gnn_a1, L0_gnn_a2, s1_rows),
        lambda: lower_slope_sums(nc, k, gat),
        lambda: attention_heads(nc, k, gat, s1_rows),
        lambda: attention_output(nc, k, x, L0_gnn_W_out, L0_gnn_b_out),
        lambda: normalised_sum(nc, k, adj, x1),
        lambda: sum_and_normalise(nc, k, "l1", x1, None, x2, True),
        lambda: logit_factors(nc, k, 0, kT, Xf[0], Xa[0], L2_gnn_W1, L2_gnn_W2, L2_gnn_W3, q_rows),
        lambda: nucleus_step(nc, k, 0, kT, q_rows, Xa[1], Xf),
        lambda: logit_factors(nc, k, 1, kT, None, Xa[1], L2_gnn_W1, L2_gnn_W2, L2_gnn_W3, q_rows),
        lambda: nucleus_step(nc, k, 1, kT, q_rows, Xa[2], Xf),
        lambda: combine_steps(nc, k, x2, Xf, Xa, (L2_gnn_U1_0, L2_gnn_U1_1), (L2_gnn_U2_0, L2_gnn_U2_1),
                              L2_gnn_gamma, L2_gnn_beta, x3),
        lambda: support(nc, k, x3, L3_gnn_weight),
        lambda: sum_and_normalise(nc, k, "l3", x3, L3_gnn_bias, out, False),
    ]
    for phase in phases[:upto]:
        before = nc.snapshot_sems()
        phase()
        nc.clear_and_free_semaphores(nc.allocated_since(before))
        nc.all_engine_barrier()


NAMES = ["x", "adj", "adjT", "L0_gnn_W_seq", "L0_gnn_a1", "L0_gnn_a2", "L0_gnn_W_out", "L0_gnn_b_out", "L2_gnn_W1",
         "L2_gnn_W2", "L2_gnn_W3", "L2_gnn_U1_0", "L2_gnn_U1_1", "L2_gnn_U2_0", "L2_gnn_U2_1", "L2_gnn_gamma",
         "L2_gnn_beta", "L3_gnn_weight", "L3_gnn_bias"]


def kernel(**inputs):
    import concourse.bacc as bacc
    from concourse.bass_utils import run_bass_kernel_spmd

    given = dict(inputs, adjT=np.asarray(inputs["adj"]).T)
    nc = bacc.Bacc("TRN2", target_bir_lowering=False, num_devices=1)
    arrays, args = {}, {}
    for name in NAMES:
        a = np.ascontiguousarray(given[name])
        arrays[f"in_{name}"] = a
        args[name] = nc.dram_tensor(f"in_{name}", a.shape, mybir.dt.from_np(a.dtype), kind="ExternalInput").ap()
    out = nc.dram_tensor("out_rows", (N, D), F32, kind="ExternalOutput").ap()
    build(nc, out=out, **args)
    result = run_bass_kernel_spmd(nc, [arrays], core_ids=[0])
    return result.results[0]["out_rows"]
```
